# Optimizing a Trainium2 kernel written in Bass

```python
import numpy as np
import jax
import jax.numpy as jnp

def _softmax(x, axis=-1):
    return jax.nn.softmax(x, axis=axis)

def _gelu(x):
    return jax.nn.gelu(x, approximate=True)

def _silu(x):
    return jax.nn.silu(x)

def _sigmoid(x):
    return jax.nn.sigmoid(x)

def _layernorm(x, axis=-1, eps=1e-05):
    m = jnp.mean(x, axis=axis, keepdims=True)
    v = jnp.var(x, axis=axis, keepdims=True)
    return (x - m) / jnp.sqrt(v + eps)

def _scatter_add(tgt, idx, src, axis=0):
    return tgt.at[idx].add(src)

def _segment_sum(src, seg, n):
    return jax.ops.segment_sum(src, seg, n)
kernel_name = 'mk_prb_d1_jaxref_r8_114a4e'

def setup_inputs(seed: int=0):
    np.random.seed(seed)
    _w = jnp.asarray

    def _L0_attn_setup():
        import jax, jax.numpy as jnp
        import numpy as np
        N_HEADS = 16
        HEAD_DIM = 128
        ROPE_BASE = 10000.0

        def _apply_rope(x, start_pos):
            B, T, H, Dh = x.shape
            half = Dh // 2
            inv_freq = 1.0 / ROPE_BASE ** (jnp.arange(0, Dh, 2, dtype=jnp.float32) / Dh)
            pos = jnp.arange(T, dtype=jnp.float32) + start_pos
            ang = pos[:, None] * inv_freq[None, :]
            cos = jnp.cos(ang)[None, :, None, :].astype(x.dtype)
            sin = jnp.sin(ang)[None, :, None, :].astype(x.dtype)
            x1 = x[..., 0::2]
            x2 = x[..., 1::2]
            r1 = x1 * cos - x2 * sin
            r2 = x1 * sin + x2 * cos
            return jnp.stack([r1, r2], axis=-1).reshape(B, T, H, Dh)
        key = jax.random.key(seed)
        k0, k1, k2, k3, k4 = jax.random.split(key, 5)
        B, T, D = (2, 256, 256)
        d_lat = 128
        x = jax.random.normal(k0, (B, T, D), dtype=jnp.float32)
        wq = jax.random.normal(k1, (D, N_HEADS * HEAD_DIM), dtype=jnp.float32) / np.sqrt(D)
        w_down = jax.random.normal(k2, (D, d_lat), dtype=jnp.float32) / np.sqrt(D)
        w_up = jax.random.normal(k3, (d_lat, 2 * N_HEADS * HEAD_DIM), dtype=jnp.float32) / np.sqrt(d_lat)
        wo = jax.random.normal(k4, (N_HEADS * HEAD_DIM, D), dtype=jnp.float32) / np.sqrt(N_HEADS * HEAD_DIM)
        return {'x': x, 'wq': wq, 'w_down': w_down, 'w_up': w_up, 'wo': wo}
    _L0_attn_in = _L0_attn_setup()

    def _L0_ffn_setup():
        import jax, jax.numpy as jnp
        import numpy as np
        B, S, D = (2, 256, 256)
        E, H, TOP_K = (8, 176, 2)
        SH = 176
        ROUTED_SCALE = 2.5
        key = jax.random.key(seed)
        ks = jax.random.split(key, 8)
        std = 0.02
        return {'x': jax.random.normal(ks[0], (B, S, D), jnp.float32), 'gate_w': jax.random.normal(ks[1], (E, D), jnp.float32) * std, 'w1': jax.random.normal(ks[2], (E, D, H), jnp.float32) * std, 'w3': jax.random.normal(ks[3], (E, D, H), jnp.float32) * std, 'w2': jax.random.normal(ks[4], (E, H, D), jnp.float32) * std, 'sw1': jax.random.normal(ks[5], (D, SH), jnp.float32) * std, 'sw3': jax.random.normal(ks[6], (D, SH), jnp.float32) * std, 'sw2': jax.random.normal(ks[7], (SH, D), jnp.float32) * std}
    _L0_ffn_in = _L0_ffn_setup()
    _d = {'L0_attn_x': _L0_attn_in['x'], 'L0_attn_wq': _L0_attn_in['wq'], 'L0_attn_w_down': _L0_attn_in['w_down'], 'L0_attn_w_up': _L0_attn_in['w_up'], 'L0_attn_wo': _L0_attn_in['wo'], 'L0_ffn_gate_w': _L0_ffn_in['gate_w'], 'L0_ffn_w1': _L0_ffn_in['w1'], 'L0_ffn_w2': _L0_ffn_in['w2'], 'L0_ffn_w3': _L0_ffn_in['w3'], 'L0_ffn_sw1': _L0_ffn_in['sw1'], 'L0_ffn_sw2': _L0_ffn_in['sw2'], 'L0_ffn_sw3': _L0_ffn_in['sw3']}
    _x0 = _d['L0_attn_x']
    _d['L0_attn_x'] = jax.random.normal(jax.random.fold_in(jax.random.key(seed), 1), (4, 512, 256), dtype=_x0.dtype)
    del _x0
    return _d

def reference(L0_attn_x, L0_attn_wq, L0_attn_w_down, L0_attn_w_up, L0_attn_wo, L0_ffn_gate_w, L0_ffn_w1, L0_ffn_w2, L0_ffn_w3, L0_ffn_sw1, L0_ffn_sw2, L0_ffn_sw3):

    def _L0_attn_ref(x, wq, w_down, w_up, wo):
        import jax, jax.numpy as jnp
        import numpy as np
        N_HEADS = 16
        HEAD_DIM = 128
        ROPE_BASE = 10000.0

        def _apply_rope(x, start_pos):
            B, T, H, Dh = x.shape
            half = Dh // 2
            inv_freq = 1.0 / ROPE_BASE ** (jnp.arange(0, Dh, 2, dtype=jnp.float32) / Dh)
            pos = jnp.arange(T, dtype=jnp.float32) + start_pos
            ang = pos[:, None] * inv_freq[None, :]
            cos = jnp.cos(ang)[None, :, None, :].astype(x.dtype)
            sin = jnp.sin(ang)[None, :, None, :].astype(x.dtype)
            x1 = x[..., 0::2]
            x2 = x[..., 1::2]
            r1 = x1 * cos - x2 * sin
            r2 = x1 * sin + x2 * cos
            return jnp.stack([r1, r2], axis=-1).reshape(B, T, H, Dh)
        B, T, D = x.shape
        H, Dh = (N_HEADS, HEAD_DIM)
        scale = Dh ** (-0.5)
        q = (x @ wq).reshape(B, T, H, Dh)
        c_kv = x @ w_down
        kv_up = (c_kv @ w_up).reshape(B, T, H, 2 * Dh)
        k, v = (kv_up[..., :Dh], kv_up[..., Dh:])
        q = _apply_rope(q, 0)
        k = _apply_rope(k, 0)
        scores = jnp.einsum('bqhd,bkhd->bhqk', q, k) * scale
        causal = jnp.tril(jnp.ones((T, T), dtype=bool))
        scores = jnp.where(causal[None, None, :, :], scores, jnp.float32(-jnp.inf))
        attn = jax.nn.softmax(scores, axis=-1)
        out = jnp.einsum('bhqk,bkhd->bqhd', attn, v).reshape(B, T, H * Dh)
        return out @ wo

    def _L0_ffn_ref(x, gate_w, w1, w2, w3, sw1, sw2, sw3):
        import jax, jax.numpy as jnp
        import numpy as np
        B, S, D = (2, 256, 256)
        E, H, TOP_K = (8, 176, 2)
        SH = 176
        ROUTED_SCALE = 2.5
        b, s, d = x.shape
        xt = x.reshape(b * s, d)
        scores = jax.nn.sigmoid(xt @ gate_w.T)
        top_scores, top_idx = jax.lax.top_k(scores, TOP_K)
        top_scores = top_scores / (jnp.sum(top_scores, axis=-1, keepdims=True) + 1e-20)
        top_scores = top_scores * ROUTED_SCALE
        combine = jnp.sum(jax.nn.one_hot(top_idx, E, dtype=xt.dtype) * top_scores[..., None], axis=1)
        h = jnp.einsum('td,edh->eth', xt, w1)
        u = jnp.einsum('td,edh->eth', xt, w3)
        y = jnp.einsum('eth,ehd->etd', jax.nn.silu(h) * u, w2)
        routed = jnp.einsum('etd,te->td', y, combine)
        shared = jax.nn.silu(xt @ sw1) * (xt @ sw3) @ sw2
        return (routed + shared).reshape(b, s, d)
    x = L0_attn_x
    xn = _layernorm(x, axis=-1)
    x = x + _L0_attn_ref(xn, L0_attn_wq, L0_attn_w_down, L0_attn_w_up, L0_attn_wo) + _L0_ffn_ref(xn, L0_ffn_gate_w, L0_ffn_w1, L0_ffn_w2, L0_ffn_w3, L0_ffn_sw1, L0_ffn_sw2, L0_ffn_sw3)
    return x

_drawn_inputs = setup_inputs


def setup_inputs(seed=0):
    import zlib

    import numpy as np

    out = dict(_drawn_inputs(seed))
    spreads = {}
    factors = {'L0_ffn_gate_w': 11.015,
     'L0_ffn_sw1': 4.159,
     'L0_ffn_sw2': 4.117,
     'L0_ffn_sw3': 4.12,
     'L0_ffn_w1': 3.604,
     'L0_ffn_w2': 3.566,
     'L0_ffn_w3': 3.572}
    for name, (base, spread) in spreads.items():
        noise = np.random.default_rng([zlib.crc32(name.encode()), seed]).standard_normal(out[name].shape)
        drawn = base * np.exp(spread * noise) if base else spread * noise
        out[name] = jnp.asarray(drawn.astype(out[name].dtype))
    for name, factor in factors.items():
        out[name] = (out[name] * factor).astype(out[name].dtype)
    return out
```

```python
from contextlib import ExitStack

import concourse.bass as bass
import numpy as np
from concourse import mybir

B, T, D = 4, 512, 256
H, DH, DL = 16, 128, 128
E, HID, TOP_K = 8, 176, 2
ROUTED_SCALE = 2.5
ROPE_BASE = 10000.0
EPS = 1e-5
SCALE = DH ** -0.5
P = 128
KD = D // P
NT = T // P
TT = B * NT
PAIRS = H // 2
HIDDEN = (E + 1) * HID
HTILES = -(-HIDDEN // P)
FPAIRS = -(-HTILES // 2)
SLOTS = H * B
BODY = 16
LOOPS = 3
LEAD = 3
CPARTS = 3
BIG = 1e30

F32 = mybir.dt.float32
F32R = mybir.dt.float32r
BF16 = mybir.dt.bfloat16
U16 = mybir.dt.uint16
U32 = mybir.dt.uint32
ALU = mybir.AluOpType
ACT = mybir.ActivationFunctionType

WQ, WK, WUV, WO = 0, 512, 768, 1024
ATTN_COLS = 1536
W1, W3, W2 = 0, 512, 1024
FFN_COLS = 1536
PT_AT = [0, 512, 896, 1152]
PR_AT = [0, 128, 384, 768]
PROBS = 1280


def ffn_of(m):
    if m < 8 * (HTILES // 2):
        return m
    if m < 8 * FPAIRS and m % 2 == 0:
        return 8 * (HTILES // 2) + (m - 8 * (HTILES // 2)) // 2
    return None


def moe_attention_kernel(nc, x_d, attn_d, ffn_d, wdown_d, gate_d, cos_d, sin_d, mask_d, ident_d,
                         iota_d, sel_d, out_d):
    with ExitStack() as ctx:
        def sb(name, shape, dt=F32):
            return ctx.enter_context(nc.sbuf_tensor(name, shape, dt))

        def ps(name, shape):
            return ctx.enter_context(nc.psum_tensor(name, shape, F32))

        def sem(name):
            return ctx.enter_context(nc.semaphore(name))

        acc = sb("acc", [P, TT, D])
        xn_hi = sb("xn_hi", [P, KD, B * T], F32R)
        xn_lo = sb("xn_lo", [P, KD, B * T], F32R)
        ct_hi = sb("ct_hi", [P, B * T], F32R)
        ct_lo = sb("ct_lo", [P, B * T], F32R)
        c_hi = sb("c_hi", [P, TT, DL], F32R)
        c_lo = sb("c_lo", [P, TT, DL], F32R)
        combT = sb("combT", [CPARTS * (E + 1), B * T], BF16)
        cos_t = sb("cos_t", [P, T])
        sin_t = sb("sin_t", [P, T])
        mask = sb("mask", [P, T])
        ident = sb("ident", [P, P])
        raw_a = sb("raw_a", [P, ATTN_COLS])
        raw_f = sb("raw_f", [P, FFN_COLS])
        wa_hi = sb("wa_hi", [P, 2, WUV], F32R)
        wa_lo = sb("wa_lo", [P, 2, WUV], F32R)
        m_hi = sb("m_hi", [P, 2, 2 * D], F32R)
        m_lo = sb("m_lo", [P, 2, 2 * D], F32R)
        wf_hi = sb("wf_hi", [P, 2, FFN_COLS], F32R)
        wf_lo = sb("wf_lo", [P, 2, FFN_COLS], F32R)
        sel = sb("sel", [CPARTS * (E + 1), 2, 2 * P], U16)
        qk_hi = sb("qk_hi", [P, 2, 2, T], F32R)
        qk_lo = sb("qk_lo", [P, 2, 2, T], F32R)
        swapped = sb("swapped", [P, 2, T])
        rot = sb("rot", [P, 2, T])
        probs = sb("probs", [P, 2, PROBS])
        pt_hi = sb("pt_hi", [P, PROBS], F32R)
        pt_lo = sb("pt_lo", [P, PROBS], F32R)
        u_hi = sb("u_hi", [P, T], F32R)
        u_lo = sb("u_lo", [P, T], F32R)
        th = sb("th", [P, T])
        act = sb("act", [P, T])
        g_hi = sb("g_hi", [P, T], F32R)
        g_lo = sb("g_lo", [P, T], F32R)
        nbias = sb("nbias", [P, 2, NT])
        sums = sb("sums", [P, 2, NT])
        rsum = sb("rsum", [P, 2, NT])
        bn = sb("bn", [P, TT, 6])
        mv = sb("mv", [P, TT, 2])
        std = sb("std", [P, TT])
        rstd = sb("rstd", [P, 3, TT])
        gate_r = sb("gate_r", [P, KD, E])
        gate = sb("gate", [P, KD, 2 * E], F32R)
        iota = sb("iota", [P, E])
        top = sb("top", [P, TT, 8])
        topi = sb("topi", [P, TT, 8], U32)
        topf = sb("topf", [P, TT, 2])
        tsum = sb("tsum", [P, 2, TT])
        topw = sb("topw", [P, TT, 2])
        partb = sb("partb", [P, TT, CPARTS * (E + 1)], BF16)

        s_bank = [ps(f"scores{i}", [P, T]) for i in range(2)]
        pt_bank = ps("probs_t", [P, T])
        u_bank = ps("u_acc", [P, T])
        qk_bank = ps("qk_proj", [P, T])
        f_bank = ps("ffn", [P, T])
        out_bank = ps("out_acc", [P, NT, D])
        out_flat = out_bank[:, :, :].rearrange("p i d -> p (i d)")

        ld_x, ld_const = [sem(f"ld_x{b}") for b in range(B)], sem("ld_const")
        ld_a, ld_f = sem("ld_a"), sem("ld_f")
        st_out = sem("st_out")
        stats, var_ok, std_ok, rstd_ok = sem("stats"), sem("var_ok"), sem("std_ok"), sem("rstd_ok")
        xn_ok, xt_ok, xhi_ok, xlo_ok = sem("xn_ok"), sem("xt_ok"), sem("xhi_ok"), sem("xlo_ok")
        wd_hi_ok, wd_lo_ok = sem("wd_hi_ok"), sem("wd_lo_ok")
        ct_ok, craw_ok, cthi_ok, ctlo_ok = sem("ct_ok"), sem("craw_ok"), sem("cthi_ok"), sem("ctlo_ok")
        c_ok, chi_ok, clo_ok = sem("c_ok"), sem("chi_ok"), sem("clo_ok")
        logit_ok, lcopy_ok, sig_ok, tanh_ok = sem("logit_ok"), sem("lcopy_ok"), sem("sig_ok"), sem("tanh_ok")
        gate_step, part_ok, partT_ok, comb_ok = sem("gate_step"), sem("part_ok"), sem("partT_ok"), sem("comb_ok")
        wa_hi_ok, wa_lo_ok = sem("wa_hi_ok"), sem("wa_lo_ok")
        wf_hi_ok, wf_lo_ok = sem("wf_hi_ok"), sem("wf_lo_ok")
        m_ok, m_hi_ok, m_lo_ok = sem("m_ok"), sem("m_hi_ok"), sem("m_lo_ok")
        proj_ok, swap_ok, cosm_ok, sinm_ok = sem("proj_ok"), sem("swap_ok"), sem("cosm_ok"), sem("sinm_ok")
        rot_ok, rhi_ok, rlo_ok = sem("rot_ok"), sem("rhi_ok"), sem("rlo_ok")
        score_ok, max_ok, exp_ok, rsum_ok, prob_ok = (sem("score_ok"), sem("max_ok"), sem("exp_ok"),
                                                      sem("rsum_ok"), sem("prob_ok"))
        pt_ok, pthi_ok, ptlo_ok = sem("pt_ok"), sem("pthi_ok"), sem("ptlo_ok")
        u_ok, uhi_ok, ulo_ok = sem("u_ok"), sem("uhi_ok"), sem("ulo_ok")
        d_done, y_done, out_free = sem("d_done"), sem("y_done"), sem("out_free")
        h_ok, tanh_h_ok, gated_ok = sem("h_ok"), sem("tanh_h_ok"), sem("gated_ok")
        up_ok, upm_ok, cw_ok, g_ok = sem("up_ok"), sem("upm_ok"), sem("cw_ok"), sem("g_ok")
        ghi_ok, glo_ok = sem("ghi_ok"), sem("glo_ok")
        scores_seen = sem("scores_seen")
        N_CONST = 7

        wd_hi = pt_hi[:, 0:D].rearrange("p (k n) -> p k n", k=KD)
        wd_lo = pt_lo[:, 0:D].rearrange("p (k n) -> p k n", k=KD)
        wd_r = th[:, 0:D].rearrange("p (k n) -> p k n", k=KD)
        xn = probs[:, :, 0:4 * D].rearrange("p a (t d) -> p a t d", d=D)
        craw = swapped
        score = th[:, D:].rearrange("p (t e) -> p t e", t=TT)
        comb = probs[:, :, 4 * D:4 * D + TT * (E + 1)].rearrange("p k (t e) -> p k t e", t=TT)
        part = act[:, 0:TT * CPARTS * (E + 1)].rearrange("p (t e) -> p t e", t=TT)

        def f32(ap):
            return ap.bitcast(F32)

        def need(eng, semaphore, value, fused=True):
            if isinstance(value, int):
                if value > 0:
                    eng.wait_ge(semaphore, value)
                return
            eng.wait_ge(semaphore, value)
            if not fused:
                eng.sem_inc(scores_seen)

        def run_slots(eng, slot):
            for s in range(-LEAD, 0):
                slot(0, s)
            with eng.Fori(0, LOOPS) as it:
                for s in range(BODY):
                    slot(it, s)
            for s in range(LOOPS * BODY, SLOTS):
                slot(0, s)

        def exists(it, m):
            return True if not isinstance(it, int) else 0 <= m < SLOTS

        def ffn(it, m):
            if not isinstance(it, int):
                return m
            return ffn_of(m) if exists(it, m) else None

        def at(it, per_slot, m):
            return it * (BODY * per_slot) + m * per_slot

        def pair_at(it, q):
            return it * 2 + q

        def prep(it, s):
            q, r = s // 8 + 1, s % 8
            if s < 0 or (isinstance(it, int) and q >= PAIRS):
                return None, None
            return q, r

        block = ctx.enter_context(nc.Block())

        @block.sync
        def _(sp):
            sp.dma_start(ident[:, :], ident_d).then_inc(ld_const, 16)
            for b in range(B):
                sp.dma_start(acc[:, NT * b:NT * b + NT, :],
                             x_d[b].rearrange("(i p) d -> p i d", p=P)).then_inc(ld_x[b], 16)
            sp.dma_start(wd_r, wdown_d.rearrange("(k p) n -> p k n", p=P)).then_inc(ld_const, 16)
            sp.dma_start(gate_r[:, :, :], gate_d.rearrange("(k p) n -> p k n", p=P)).then_inc(ld_const, 16)
            sp.dma_start(iota[:, :], iota_d).then_inc(ld_const, 16)
            sp.dma_start(raw_a[:, :], attn_d[0]).then_inc(ld_a, 16)
            sp.dma_start(cos_t[:, :], cos_d).then_inc(ld_const, 16)
            sp.dma_start(sin_t[:, :], sin_d).then_inc(ld_const, 16)
            sp.dma_start(mask[:, :], mask_d).then_inc(ld_const, 16)
            sp.dma_start(raw_f[:, :], ffn_d[0]).then_inc(ld_f, 16)
            sp.dma_start(sel[:, 0, :], sel_d[0]).then_inc(ld_f, 16)

            def attn_weights(p):
                sp.wait_ge(wa_hi_ok, p + 1)
                sp.wait_ge(wa_lo_ok, p + 1)
                sp.wait_ge(m_ok, p + 1)
                sp.dma_start(raw_a[:, :], attn_d[bass.ds(p + 1, 1)].rearrange("a p n -> p (a n)")).then_inc(ld_a, 16)

            def ffn_weights(p, parity):
                sp.wait_ge(wf_hi_ok, p + 1)
                sp.wait_ge(wf_lo_ok, p + 1)
                sp.dma_start(raw_f[:, :], ffn_d[bass.ds(p + 1, 1)].rearrange("a p n -> p (a n)")).then_inc(ld_f, 16)
                sp.wait_ge(cw_ok, 8 * p + 1)
                sp.dma_start(sel[:, parity, :], sel_d[bass.ds(p + 1, 1)].rearrange("a p n -> p (a n)")).then_inc(ld_f, 16)

            with sp.Fori(0, LOOPS) as it:
                for q in range(2):
                    attn_weights(it * 2 + q)
                    ffn_weights(it * 2 + q, (q + 1) % 2)
            attn_weights(2 * LOOPS)
            for b in range(B):
                sp.wait_ge(out_free, 1 + B * (PAIRS - 1) + b + 1)
                sp.dma_start(out_d[b].rearrange("(i p) d -> p i d", p=P),
                             acc[:, NT * b:NT * b + NT, :]).then_inc(st_out, 16)
            sp.wait_ge(st_out, 16 * B)

        @block.tensor
        def _(pe):
            def product(out, pairs, start, stop, **kw):
                n = 0
                for (a_hi, a_lo), (b_hi, b_lo) in pairs:
                    for a, b in ((a_hi, b_hi), (a_hi, b_lo), (a_lo, b_hi)):
                        last = pe.matmul(out, a, b, start=start and n == 0,
                                         stop=stop and n == 3 * len(pairs) - 1, **kw)
                        n += 1
                return last

            def value_output(parity):
                for hp in range(2):
                    last = pe.matmul(qk_bank[:, hp * D:hp * D + D], raw_a[:, WUV + hp * DL:WUV + hp * DL + DL],
                                     raw_a[:, WO + hp * D:WO + hp * D + D], start=True, stop=True)
                last.then_inc(m_ok, 1)

            pe.wait_ge(ld_const, 16 * N_CONST)
            banks = [s_bank, [pt_bank, qk_bank]]
            for b in range(B):
                for i in range(NT):
                    t = NT * b + i
                    pe.wait_ge(xn_ok, t + 1)
                    if b >= 2 and i == 0:
                        pe.wait_ge(xhi_ok, KD * (b - 1))
                        pe.wait_ge(xlo_ok, KD * (b - 1))
                    for k in range(KD):
                        last = pe.transpose(banks[b % 2][k][:, i * P:i * P + P],
                                            xn[:, t // 4 % 2, t % 4, k * P:k * P + P], ident[:, :])
                    last.then_inc(xt_ok, 1)
            pe.wait_ge(wd_hi_ok, 2)
            pe.wait_ge(wd_lo_ok, 2)
            for b in range(B):
                pe.wait_ge(xhi_ok, KD * (b + 1))
                pe.wait_ge(xlo_ok, KD * (b + 1))
                pe.wait_ge(cthi_ok, b) if b else None
                pe.wait_ge(ctlo_ok, b) if b else None
                product(u_bank[:, :], [((wd_hi[:, k, :], wd_lo[:, k, :]),
                                        (xn_hi[:, k, b * T:b * T + T], xn_lo[:, k, b * T:b * T + T]))
                                       for k in range(KD)], True, True).then_inc(ct_ok, 1)
                for i in range(NT):
                    t = NT * b + i
                    for n, (a, k) in enumerate((a, k) for a in (xn_hi, xn_lo) for k in range(KD)):
                        last = pe.matmul(f_bank[:, t * 2 * E:(t + 1) * 2 * E], a[:, k, t * P:t * P + P],
                                         gate[:, k, :], start=n == 0, stop=n == 3)
                last.then_inc(logit_ok, 1)
                pe.wait_ge(craw_ok, b + 1)
                if b:
                    pe.wait_ge(chi_ok, b)
                    pe.wait_ge(clo_ok, b)
                for i in range(NT):
                    last = pe.transpose(out_flat[:, i * P:i * P + P], craw[:, b % 2, i * P:i * P + P], ident[:, :])
                last.then_inc(c_ok, 1)
            pe.wait_ge(ld_a, 16)
            value_output(0)
            for b in range(B):
                pe.wait_ge(part_ok, 1)
                if b:
                    pe.wait_ge(comb_ok, b)
                for i in range(NT):
                    last = pe.transpose(out_flat[0:CPARTS * (E + 1), T + i * P:T + i * P + P],
                                        part[:, NT * b + i, :], ident[:, :])
                last.then_inc(partT_ok, 1)
            pe.wait_ge(comb_ok, B)
            pe.wait_ge(chi_ok, B)
            pe.wait_ge(clo_ok, B)
            pe.wait_ge(ctlo_ok, B)
            pe.wait_ge(m_hi_ok, 1)
            pe.wait_ge(m_lo_ok, 1)

            def where(m):
                return (m // 8) % 2, (m % 8) // 2, m % 2

            def x_of(b):
                return [(xn_hi[:, k, b * T:b * T + T], xn_lo[:, k, b * T:b * T + T]) for k in range(KD)]

            def project(it, m, which):
                if not exists(it, m):
                    return
                par, b, hp = where(m)
                if m % 8 == 0 and which == 0:
                    need(pe, wa_hi_ok, pair_at(it, m // 8) + 1)
                    need(pe, wa_lo_ok, pair_at(it, m // 8) + 1)
                need(pe, swap_ok, at(it, 2, m) + which)
                need(pe, cosm_ok, at(it, 2, m) + which)
                if which == 0:
                    c = hp * DH
                    prods = [((wa_hi[:, par, WQ + 256 * k + c:WQ + 256 * k + c + DH],
                               wa_lo[:, par, WQ + 256 * k + c:WQ + 256 * k + c + DH]), x_of(b)[k])
                             for k in range(KD)]
                else:
                    c = WK + hp * DH
                    prods = [((wa_hi[:, par, c:c + DH], wa_lo[:, par, c:c + DH]),
                              (ct_hi[:, b * T:b * T + T], ct_lo[:, b * T:b * T + T]))]
                product(qk_bank[:, :], prods, True, True).then_inc(proj_ok, 1)

            def scores(it, m, i):
                if not exists(it, m):
                    return
                k = NT - 1 - i
                if k == 0:
                    need(pe, rhi_ok, at(it, 2, m + 1))
                    need(pe, rlo_ok, at(it, 2, m + 1))
                need(pe, exp_ok, at(it, 4, m) + k - 1)
                q, n = (m % 2, 0, slice(i * P, i * P + P)), (i + 1) * P
                product(s_bank[i % 2][:, 0:n],
                        [((qk_hi[:, q[0], 0, q[2]], qk_lo[:, q[0], 0, q[2]]),
                          (qk_hi[:, m % 2, 1, 0:n], qk_lo[:, m % 2, 1, 0:n]))], True, True).then_inc(score_ok, 1)

            def transposes(it, m, j):
                if not exists(it, m):
                    return
                if j == 0:
                    need(pe, prob_ok, at(it, 4, m + 1))
                need(pe, ptlo_ok, at(it, 4, m) + j)
                for i in range(j, NT):
                    a = PR_AT[i] + j * P
                    last = pe.transpose(pt_bank[:, (i - j) * P:(i - j + 1) * P], probs[:, m % 2, a:a + P],
                                        ident[:, :])
                last.then_inc(pt_ok, 1)

            def weighted(it, m, j):
                if not exists(it, m):
                    return
                if j == 0:
                    need(pe, uhi_ok, at(it, 1, m))
                    need(pe, ulo_ok, at(it, 1, m))
                need(pe, ptlo_ok, at(it, 4, m) + j + 1)
                _, b, _ = where(m)
                t, a, n = NT * b + j, PT_AT[j], T - j * P
                last = product(u_bank[:, j * P:T], [((c_hi[:, t, :], c_lo[:, t, :]),
                                                     (pt_hi[:, a:a + n], pt_lo[:, a:a + n]))], j == 0, j == NT - 1)
                if j == NT - 1:
                    last.then_inc(u_ok, 1)

            def out_products(parts, w_hi, w_lo, opens):
                a_hi, a_lo = parts
                for i in range(NT):
                    t = slice(i * P, i * P + P)
                    last = product(out_bank[:, i, :], [((a_hi[:, t], a_lo[:, t]), (w_hi, w_lo))],
                                   opens and i % 2 == 0, False, skip_group_check=True)
                return last

            def outputs(it, s):
                par, b, hp = where(s)
                even = s % 2 == 0
                f = ffn(it, s)

                def y():
                    if f is None:
                        return
                    need(pe, ghi_ok, at(it, 1, f + 1))
                    need(pe, glo_ok, at(it, 1, f + 1))
                    c = W2 + hp * D
                    out_products((g_hi, g_lo), wf_hi[:, par, c:c + D], wf_lo[:, par, c:c + D],
                                 False).then_inc(y_done, 1)

                def d():
                    if not exists(it, s):
                        return
                    if even:
                        need(pe, out_free, it * (BODY // 2) + s // 2 + 1)
                    if s % 8 == 0:
                        need(pe, m_hi_ok, pair_at(it, s // 8) + 1)
                        need(pe, m_lo_ok, pair_at(it, s // 8) + 1)
                    need(pe, uhi_ok, at(it, 1, s + 1))
                    need(pe, ulo_ok, at(it, 1, s + 1))
                    last = out_products((u_hi, u_lo), m_hi[:, par, hp * D:hp * D + D],
                                        m_lo[:, par, hp * D:hp * D + D], even)
                    last.then_inc(d_done, 1)
                return y, d

            def hidden(it, m, which):
                f = ffn(it, m)
                if f is None:
                    return
                par, b, hp = where(m)
                if m % 8 == 0 and which == 0:
                    need(pe, wf_hi_ok, pair_at(it, m // 8) + 1)
                    need(pe, wf_lo_ok, pair_at(it, m // 8) + 1)
                need(pe, g_ok, at(it, 1, f)) if which == 0 else need(pe, gated_ok, at(it, 1, f + 1))
                c = (W1, W3)[which] + hp * P
                product(f_bank[:, :], [((wf_hi[:, par, c + 256 * k:c + 256 * k + P],
                                         wf_lo[:, par, c + 256 * k:c + 256 * k + P]), x_of(b)[k])
                                       for k in range(KD)], True, True).then_inc((h_ok, up_ok)[which], 1)

            def combine(it, m):
                f = ffn(it, m)
                if f is None:
                    return
                par, b, hp = where(m)
                if m % 8 == 0:
                    need(pe, ld_f, pair_at(it, m // 8) * 32 + 32)
                need(pe, upm_ok, at(it, 1, f + 1))
                pe.matmul(f_bank[:, :], sel[:, par, hp * P:hp * P + P].bitcast(BF16),
                          combT[:, b * T:b * T + T], start=True, stop=True).then_inc(cw_ok, 1)

            def slot(it, s):
                y, d = outputs(it, s)
                q, r = prep(it, s)
                transposes(it, s + 1, 0)
                if r == 4:
                    need(pe, m_hi_ok, pair_at(it, q) + 1)
                    need(pe, m_lo_ok, pair_at(it, q) + 1)
                project(it, s + 3, 0)
                scores(it, s + 2, 3)
                combine(it, s)
                weighted(it, s + 1, 0)
                transposes(it, s + 1, 1)
                d()
                scores(it, s + 2, 2)
                weighted(it, s + 1, 1)
                transposes(it, s + 1, 2)
                project(it, s + 3, 1)
                scores(it, s + 2, 1)
                hidden(it, s + 1, 0)
                weighted(it, s + 1, 2)
                transposes(it, s + 1, 3)
                scores(it, s + 2, 0)
                y()
                if r == 3:
                    need(pe, cosm_ok, at(it, 2, s + 4))
                    need(pe, ld_a, (pair_at(it, q) + 1) * 16)
                    value_output(q % 2)
                hidden(it, s + 1, 1)
                weighted(it, s + 1, 3)

            run_slots(pe, slot)

        @block.scalar
        def _(ac):
            def m_parts(p_count, parity):
                need(ac, m_ok, p_count)
                ac.activation(m_hi[:, parity, :], qk_bank[:, :], ACT.Copy).then_inc(m_hi_ok, 1)

            ac.wait_ge(ld_const, 16 * N_CONST)
            ac.activation(wd_hi, wd_r, ACT.Copy).then_inc(wd_hi_ok, 1)
            ac.activation(gate[:, :, 0:E], gate_r[:, :, :], ACT.Copy).then_inc(wd_hi_ok, 1)
            ac.wait_ge(var_ok, 1)
            ac.activation(std[:, :], rstd[:, 0, :], ACT.Sqrt).then_inc(std_ok, 1)
            banks = [s_bank, [pt_bank, qk_bank]]
            for b in range(B):
                ac.wait_ge(xt_ok, NT * (b + 1))
                for k in range(KD):
                    ac.activation(xn_hi[:, k, b * T:b * T + T], banks[b % 2][k][:, :], ACT.Copy).then_inc(xhi_ok, 1)
            for b in range(B):
                ac.wait_ge(ct_ok, b + 1)
                if b >= 2:
                    ac.wait_ge(c_ok, b - 1)
                ac.activation(craw[:, b % 2, :], u_bank[:, :], ACT.Copy).then_inc(craw_ok, 1)
                ac.activation(ct_hi[:, b * T:b * T + T], u_bank[:, :], ACT.Copy).then_inc(cthi_ok, 1)
                ac.wait_ge(c_ok, b + 1)
                ac.activation(c_hi[:, NT * b:NT * b + NT, :].rearrange("p i d -> p (i d)"),
                              out_flat[:, 0:T], ACT.Copy).then_inc(chi_ok, 1)
            ac.wait_ge(ld_a, 16)
            ac.activation(wa_hi[:, 0, :], raw_a[:, 0:WUV], ACT.Copy).then_inc(wa_hi_ok, 1)
            ac.wait_ge(ld_f, 32)
            ac.activation(wf_hi[:, 0, :], raw_f[:, :], ACT.Copy).then_inc(wf_hi_ok, 1)
            m_parts(1, 0)
            ac.wait_ge(logit_ok, B)
            ac.activation(score[:, :, :].rearrange("p t e -> p (t e)"), f_bank[:, 0:TT * 2 * E],
                          ACT.Copy).then_inc(lcopy_ok, 1)
            ac.wait_ge(sig_ok, 1)
            ac.activation(score[:, :, E:2 * E], score[:, :, 0:E], ACT.Tanh, scale=0.5).then_inc(tanh_ok, 1)
            for b in range(B):
                ac.wait_ge(partT_ok, b + 1)
                ac.activation(combT[:, b * T:b * T + T], out_flat[0:CPARTS * (E + 1), T:2 * T],
                              ACT.Copy).then_inc(comb_ok, 1)

            def swap(it, m, which):
                if not exists(it, m):
                    return
                need(ac, proj_ok, at(it, 2, m) + which + 1)
                need(ac, rot_ok, at(it, 2, m - 1) + which + 1)
                for half in range(2):
                    last = ac.activation(swapped[64 * half:64 * half + 64, which, :],
                                         qk_bank[64 - 64 * half:128 - 64 * half, :], ACT.Copy)
                last.then_inc(swap_ok, 1)

            def rot_parts(it, m, which):
                if not exists(it, m):
                    return
                need(ac, rot_ok, at(it, 2, m) + which + 1)
                need(ac, score_ok, at(it, 4, m - 1))
                ac.activation(qk_hi[:, m % 2, which, :], rot[:, which, :], ACT.Copy).then_inc(rhi_ok, 1)

            def exps(it, m, i):
                if not exists(it, m):
                    return
                k = NT - 1 - i
                need(ac, max_ok, at(it, 4, m) + k + 1)
                if k == 0:
                    need(ac, pt_ok, at(it, 4, m - 1))
                n = (i + 1) * P
                ac.activation(probs[:, m % 2, PR_AT[i]:PR_AT[i] + n], s_bank[i % 2][:, 0:n], ACT.Exp,
                              bias=nbias[:, m % 2, i:i + 1], scale=-1.0,
                              accum_out=sums[:, m % 2, i:i + 1]).then_inc(exp_ok, 1)

            def pt_parts(it, m, j):
                if not exists(it, m):
                    return
                if j == 0:
                    need(ac, u_ok, at(it, 1, m))
                need(ac, pt_ok, at(it, 4, m) + j + 1)
                n = T - j * P
                ac.activation(pt_hi[:, PT_AT[j]:PT_AT[j] + n], pt_bank[:, 0:n], ACT.Copy).then_inc(pthi_ok, 1)

            def u_parts(it, m):
                if not exists(it, m):
                    return
                need(ac, d_done, at(it, 1, m))
                need(ac, u_ok, at(it, 1, m + 1))
                ac.activation(u_hi[:, :], u_bank[:, :], ACT.Copy).then_inc(uhi_ok, 1)

            def tanh(it, m):
                f = ffn(it, m)
                if f is None:
                    return
                need(ac, gated_ok, at(it, 1, f))
                need(ac, h_ok, at(it, 1, f + 1))
                ac.activation(th[:, :], f_bank[:, :], ACT.Tanh, scale=0.5).then_inc(tanh_h_ok, 1)

            def g_parts(it, m):
                f = ffn(it, m)
                if f is None:
                    return
                need(ac, y_done, at(it, 1, f))
                need(ac, g_ok, at(it, 1, f + 1))
                ac.activation(g_hi[:, :], act[:, :], ACT.Copy).then_inc(ghi_ok, 1)

            def weights(it, s):
                q, r = prep(it, s)
                if r not in (2, 3, 4):
                    return
                if r == 2:
                    need(ac, d_done, at(it, 1, 8 * (q - 1) + 2))
                    need(ac, ld_a, (pair_at(it, q) + 1) * 16)
                    ac.activation(wa_hi[:, q % 2, :], raw_a[:, 0:WUV], ACT.Copy).then_inc(wa_hi_ok, 1)
                if r == 3:
                    m_parts(pair_at(it, q) + 1, q % 2)
                if r == 4 and (not isinstance(it, int) or q < FPAIRS):
                    need(ac, ld_f, (pair_at(it, q) + 1) * 32)
                    ac.activation(wf_hi[:, q % 2, :], raw_f[:, :], ACT.Copy).then_inc(wf_hi_ok, 1)

            def slot(it, s):
                u_parts(it, s)
                pt_parts(it, s + 1, 0)
                swap(it, s + 3, 0)
                g_parts(it, s)
                exps(it, s + 2, 3)
                pt_parts(it, s + 1, 1)
                rot_parts(it, s + 3, 0)
                exps(it, s + 2, 2)
                pt_parts(it, s + 1, 2)
                swap(it, s + 3, 1)
                exps(it, s + 2, 1)
                tanh(it, s + 1)
                pt_parts(it, s + 1, 3)
                exps(it, s + 2, 0)
                weights(it, s)
                rot_parts(it, s + 3, 1)

            run_slots(ac, slot)

        @block.gpsimd
        def _(pool):
            def parts_of(p_count_a, parity):
                need(pool, wa_hi_ok, p_count_a)
                pool.tensor_tensor(wa_lo[:, parity, :], raw_a[:, 0:WUV], f32(wa_hi[:, parity, :]),
                                   ALU.subtract).then_inc(wa_lo_ok, 1)

            def ffn_parts(part_no, parity, p_count):
                need(pool, wf_hi_ok, p_count)
                c = slice(512 * part_no, 512 * part_no + 512)
                ins = pool.tensor_tensor(wf_lo[:, parity, c], raw_f[:, c], f32(wf_hi[:, parity, c]), ALU.subtract)
                if part_no == 2:
                    ins.then_inc(wf_lo_ok, 1)

            pool.wait_ge(ld_const, 16 * N_CONST)
            parts_of(1, 0)
            for n in range(3):
                ffn_parts(n, 0, 1)

            def sin_product(it, m, which):
                if not exists(it, m):
                    return
                need(pool, swap_ok, at(it, 2, m) + which + 1)
                pool.tensor_tensor(swapped[:, which, :], swapped[:, which, :], sin_t[:, :],
                                   ALU.mult).then_inc(sinm_ok, 1)

            def rot_parts(it, m, which):
                if not exists(it, m):
                    return
                need(pool, rhi_ok, at(it, 2, m) + which + 1)
                pool.tensor_tensor(qk_lo[:, m % 2, which, :], rot[:, which, :], f32(qk_hi[:, m % 2, which, :]),
                                   ALU.subtract).then_inc(rlo_ok, 1)

            def g_parts(it, m):
                f = ffn(it, m)
                if f is None:
                    return
                need(pool, ghi_ok, at(it, 1, f + 1))
                pool.tensor_tensor(g_lo[:, :], act[:, :], f32(g_hi[:, :]), ALU.subtract).then_inc(glo_ok, 1)

            def weights(it, s):
                q, r = prep(it, s)
                if r == 2:
                    parts_of(pair_at(it, q) + 1, q % 2)
                if r in (4, 5, 6) and (not isinstance(it, int) or q < FPAIRS):
                    ffn_parts(r - 4, q % 2, pair_at(it, q) + 1)

            def slot(it, s):
                sin_product(it, s + 3, 0)
                g_parts(it, s)
                rot_parts(it, s + 3, 0)
                sin_product(it, s + 3, 1)
                weights(it, s)
                rot_parts(it, s + 3, 1)

            run_slots(pool, slot)

        @block.vector
        def _(ve):
            steps = [0]

            def step(ins):
                steps[0] += 1
                ins.then_inc(gate_step, 1)
                ve.wait_ge(gate_step, steps[0])

            def flat(ap):
                return ap.rearrange("p t e -> p (t e)")

            ve.memset(comb[:, :, :, :], 0.5).then_inc(out_free, 1)
            for b in range(B):
                ve.wait_ge(ld_x[b], 16)
                for t in range(NT * b, NT * b + NT):
                    last = ve.bn_stats(bn[:, t, :], acc[:, t, :])
                last.then_inc(stats, 1)
                ve.wait_ge(stats, b + 1)
                for t in range(NT * b, NT * b + NT):
                    last = ve.bn_aggr(mv[:, t, :], bn[:, t, :])
            step(last)
            step(ve.tensor_scalar(rstd[:, 0, :], mv[:, :, 1], EPS, None, ALU.add))
            ve.nop().then_inc(var_ok, 1)
            ve.wait_ge(std_ok, 1)
            step(ve.reciprocal(rstd[:, 1, :], std[:, :]))
            step(ve.tensor_tensor(rstd[:, 2, :], rstd[:, 0, :], rstd[:, 1, :], ALU.mult))
            step(ve.tensor_tensor(rstd[:, 2, :], rstd[:, 2, :], rstd[:, 1, :], ALU.mult))
            step(ve.tensor_scalar(rstd[:, 2, :], rstd[:, 2, :], -0.5, 1.5, ALU.mult, ALU.add))
            step(ve.tensor_tensor(rstd[:, 0, :], rstd[:, 2, :], rstd[:, 1, :], ALU.mult))
            banks = [s_bank, [pt_bank, qk_bank]]

            def x_low(b):
                for k in range(KD):
                    ve.wait_ge(xhi_ok, KD * b + k + 1)
                    ve.tensor_tensor(xn_lo[:, k, b * T:b * T + T], banks[b % 2][k][:, :],
                                     f32(xn_hi[:, k, b * T:b * T + T]), ALU.subtract).then_inc(xlo_ok, 1)

            for b in range(B):
                for t in range(NT * b, NT * b + NT):
                    if t >= 8:
                        ve.wait_ge(xt_ok, t - 7)
                    ve.tensor_scalar(xn[:, t // 4 % 2, t % 4, :], acc[:, t, :], mv[:, t, 0:1], rstd[:, 0, t:t + 1],
                                     ALU.subtract, ALU.mult).then_inc(xn_ok, 1)
                if b >= 1:
                    x_low(b - 1)
            x_low(B - 1)
            ve.wait_ge(wd_hi_ok, 2)
            ve.tensor_tensor(wd_lo, wd_r, f32(wd_hi), ALU.subtract).then_inc(wd_lo_ok, 1)
            ve.tensor_tensor(gate[:, :, E:2 * E], gate_r[:, :, :], f32(gate[:, :, 0:E]),
                             ALU.subtract).then_inc(wd_lo_ok, 1)
            for b in range(B):
                ve.wait_ge(cthi_ok, b + 1)
                ve.tensor_tensor(ct_lo[:, b * T:b * T + T], u_bank[:, :], f32(ct_hi[:, b * T:b * T + T]),
                                 ALU.subtract).then_inc(ctlo_ok, 1)
                ve.wait_ge(chi_ok, b + 1)
                ve.tensor_tensor(flat(c_lo[:, NT * b:NT * b + NT, :]), out_flat[:, 0:T],
                                 f32(flat(c_hi[:, NT * b:NT * b + NT, :])), ALU.subtract).then_inc(clo_ok, 1)

            def m_parts(p_count, parity):
                need(ve, m_hi_ok, p_count)
                ve.tensor_tensor(m_lo[:, parity, :], qk_bank[:, :], f32(m_hi[:, parity, :]),
                                 ALU.subtract).then_inc(m_lo_ok, 1)

            m_parts(1, 0)
            ve.wait_ge(lcopy_ok, 1)
            ve.tensor_tensor(score[:, :, 0:E], score[:, :, 0:E], score[:, :, E:2 * E],
                             ALU.add).then_inc(sig_ok, 1)
            ve.wait_ge(tanh_ok, 1)
            step(ve.tensor_scalar(score[:, :, 0:E], score[:, :, E:2 * E], 0.5, 0.5, ALU.mult, ALU.add))
            for t in range(TT):
                last = ve.max(top[:, t, :], score[:, t, 0:E])
            step(last)
            for t in range(TT):
                last = ve.max_index(topi[:, t, :], top[:, t, :], score[:, t, 0:E])
            step(last)
            step(ve.tensor_copy(topf[:, :, :], topi[:, :, 0:TOP_K]))
            step(ve.tensor_tensor(tsum[:, 0, :], top[:, :, 0], top[:, :, 1], ALU.add))
            step(ve.tensor_scalar(tsum[:, 0, :], tsum[:, 0, :], 1e-20, None, ALU.add))
            step(ve.reciprocal(tsum[:, 1, :], tsum[:, 0, :]))
            for k in range(TOP_K):
                last = ve.scalar_tensor_tensor(out=topw[:, :, k], in0=top[:, :, k], scalar=0.5 * ROUTED_SCALE,
                                               in1=tsum[:, 1, :], op0=ALU.mult, op1=ALU.mult)
            step(last)
            for t in range(TT):
                for k in range(TOP_K):
                    last = ve.tensor_scalar(comb[:, k, t, 0:E], iota[:, :], topf[:, t, k:k + 1],
                                            topw[:, t, k:k + 1], ALU.is_equal, ALU.mult)
            step(last)
            step(ve.tensor_tensor(comb[:, 0, :, 0:E], comb[:, 0, :, 0:E], comb[:, 1, :, 0:E], ALU.add))
            for n in range(CPARTS):
                c = slice(n * (E + 1), (n + 1) * (E + 1))
                step(ve.tensor_copy(partb[:, :, c], comb[:, 0, :, :]))
                step(ve.tensor_copy(part[:, :, c], partb[:, :, c]))
                step(ve.tensor_tensor(comb[:, 0, :, :], comb[:, 0, :, :], part[:, :, c], ALU.subtract))
            ve.nop().then_inc(part_ok, 1)

            def cos_product(it, m, which):
                if not exists(it, m):
                    return
                need(ve, swap_ok, at(it, 2, m) + which + 1)
                need(ve, rlo_ok, at(it, 2, m - 1) + which + 1)
                ve.tensor_tensor(rot[:, which, :], qk_bank[:, :], cos_t[:, :], ALU.mult).then_inc(cosm_ok, 1)

            def rotate(it, m, which):
                if not exists(it, m):
                    return
                need(ve, cosm_ok, at(it, 2, m) + which + 1)
                need(ve, sinm_ok, at(it, 2, m) + which + 1)
                ve.tensor_tensor(rot[:, which, :], rot[:, which, :], swapped[:, which, :],
                                 ALU.add).then_inc(rot_ok, 1)

            def row_max(it, m, i):
                if not exists(it, m):
                    return
                need(ve, score_ok, at(it, 4, m) + NT - i, fused=False)
                n = (i + 1) * P
                s = s_bank[i % 2][:, 0:n]
                ve.tensor_tensor_reduce(s, s, mask[:, T - n:T], -SCALE, 3e38, ALU.add, ALU.min,
                                        nbias[:, m % 2, i:i + 1]).then_inc(max_ok, 1)

            def invert_sum(it, m, i):
                if not exists(it, m):
                    return
                need(ve, exp_ok, at(it, 4, m) + NT - i)
                ve.reciprocal(rsum[:, m % 2, i:i + 1], sums[:, m % 2, i:i + 1]).then_inc(rsum_ok, 1)

            def normalise(it, m, i):
                if not exists(it, m):
                    return
                need(ve, rsum_ok, at(it, 4, m) + NT - i)
                a = probs[:, m % 2, PR_AT[i]:PR_AT[i] + (i + 1) * P]
                ve.tensor_scalar(a, a, rsum[:, m % 2, i:i + 1], None, ALU.mult).then_inc(prob_ok, 1)

            def pt_parts(it, m, j):
                if not exists(it, m):
                    return
                need(ve, pthi_ok, at(it, 4, m) + j + 1)
                n = T - j * P
                c = slice(PT_AT[j], PT_AT[j] + n)
                ve.tensor_tensor(pt_lo[:, c], pt_bank[:, 0:n], f32(pt_hi[:, c]), ALU.subtract).then_inc(ptlo_ok, 1)

            def u_parts(it, m):
                if not exists(it, m):
                    return
                need(ve, uhi_ok, at(it, 1, m + 1))
                ve.tensor_tensor(u_lo[:, :], u_bank[:, :], f32(u_hi[:, :]), ALU.subtract).then_inc(ulo_ok, 1)

            def gate_h(it, m):
                f = ffn(it, m)
                if f is None:
                    return
                need(ve, tanh_h_ok, at(it, 1, f + 1))
                need(ve, glo_ok, at(it, 1, f))
                ve.scalar_tensor_tensor(out=act[:, :], in0=th[:, :], scalar=1.0, in1=f_bank[:, :],
                                        op0=ALU.add, op1=ALU.mult).then_inc(gated_ok, 1)

            def times_bank(it, m, filled, before, after):
                f = ffn(it, m)
                if f is None:
                    return
                need(ve, before, at(it, 1, f + 1))
                need(ve, filled, at(it, 1, f + 1))
                ve.tensor_tensor(act[:, :], act[:, :], f_bank[:, :], ALU.mult).then_inc(after, 1)

            def add_out(it, s):
                if not exists(it, s) or s % 2 == 0:
                    return
                b = (s % 8) // 2
                need(ve, d_done, at(it, 1, s + 1))
                if ffn(it, s) is not None:
                    need(ve, y_done, at(it, 1, s + 1))
                elif ffn(it, s - 1) is not None:
                    need(ve, y_done, ffn(it, s - 1) + 1)
                need(ve, out_free, it * (BODY // 2) + s // 2 + 1)
                a = flat(acc[:, NT * b:NT * b + NT, :])
                ve.tensor_tensor(a, a, out_flat, ALU.add).then_inc(out_free, 1)

            def slot(it, s):
                q, r = prep(it, s)
                times_bank(it, s, up_ok, gated_ok, upm_ok)
                u_parts(it, s)
                pt_parts(it, s + 1, 0)
                times_bank(it, s, cw_ok, upm_ok, g_ok)
                row_max(it, s + 2, 3)
                cos_product(it, s + 3, 0)
                invert_sum(it, s + 2, 3)
                pt_parts(it, s + 1, 1)
                normalise(it, s + 2, 3)
                rotate(it, s + 3, 0)
                row_max(it, s + 2, 2)
                pt_parts(it, s + 1, 2)
                invert_sum(it, s + 2, 2)
                row_max(it, s + 2, 1)
                normalise(it, s + 2, 2)
                cos_product(it, s + 3, 1)
                invert_sum(it, s + 2, 1)
                gate_h(it, s + 1)
                normalise(it, s + 2, 1)
                pt_parts(it, s + 1, 3)
                row_max(it, s + 2, 0)
                rotate(it, s + 3, 1)
                invert_sum(it, s + 2, 0)
                normalise(it, s + 2, 0)
                add_out(it, s)
                if r == 3:
                    m_parts(pair_at(it, q) + 1, q % 2)

            run_slots(ve, slot)

def _pairs_of_heads(wq, w_up, wo):
    halves = np.concatenate([np.arange(0, DH, 2), np.arange(1, DH, 2)])
    blob = np.zeros((PAIRS, P, ATTN_COLS), wq.dtype)
    q = wq.reshape(KD, P, PAIRS, 2, DH)[..., halves]
    blob[:, :, WQ:WK] = q.transpose(2, 1, 0, 3, 4).reshape(PAIRS, P, -1)
    kv = w_up.reshape(DL, PAIRS, 2, 2, DH)
    blob[:, :, WK:WUV] = kv[:, :, :, 0, :][..., halves].transpose(1, 0, 2, 3).reshape(PAIRS, P, -1)
    blob[:, :, WUV:WO] = kv[:, :, :, 1, :].transpose(1, 3, 2, 0).reshape(PAIRS, P, -1)
    blob[:, :, WO:] = wo.reshape(PAIRS, 2, DH, D).transpose(0, 2, 1, 3).reshape(PAIRS, P, -1)
    return blob


def _pairs_of_hidden(w1, w3, w2, sw1, sw3, sw2):
    n = FPAIRS * 2 * P
    up = np.zeros((2, D, n), w1.dtype)
    down = np.zeros((n, D), w1.dtype)
    for e in range(E + 1):
        at = slice(e * HID, (e + 1) * HID)
        up[0, :, at], up[1, :, at], down[at] = (w1[e], w3[e], w2[e]) if e < E else (sw1, sw3, sw2)
    blob = np.zeros((FPAIRS, P, FFN_COLS), w1.dtype)
    u = up.reshape(2, KD, P, FPAIRS, 2 * P).transpose(3, 2, 0, 1, 4)
    blob[:, :, W1:W2] = u.reshape(FPAIRS, P, -1)
    blob[:, :, W2:] = down.reshape(FPAIRS, 2, P, D).transpose(0, 2, 1, 3).reshape(FPAIRS, P, -1)
    return blob


def _constants():
    freq = (1.0 / ROPE_BASE ** (np.arange(0, DH, 2, dtype=np.float32) / DH)).astype(np.float32)
    ang = (np.arange(T, dtype=np.float32)[None, :] * freq[:, None]).astype(np.float32)
    cos = np.concatenate([np.cos(ang), np.cos(ang)]).astype(np.float32)
    sin = np.concatenate([-np.sin(ang), np.sin(ang)]).astype(np.float32)
    mask = np.zeros((P, T), np.float32)
    mask[:, T - P:] = np.where(np.arange(P)[:, None] >= np.arange(P)[None, :], 0.0, -BIG)
    iota = np.tile(np.arange(E, dtype=np.float32), (P, 1))
    owner = np.arange(FPAIRS * 2 * P) // HID
    chosen = (owner[None, :] == np.arange(E + 1)[:, None])
    bf16_one = np.uint16(0x3F80)
    sel = np.where(np.tile(chosen, (CPARTS, 1)), bf16_one, np.uint16(0))
    sel = sel.reshape(CPARTS * (E + 1), FPAIRS, 2 * P).transpose(1, 0, 2)
    return {"cos": cos, "sin": sin, "mask": mask, "ident": np.eye(P, dtype=np.float32),
            "iota": iota, "sel": np.ascontiguousarray(sel)}


def kernel(**inputs):
    import concourse.bacc as _bacc
    from concourse.bass_utils import run_bass_kernel_spmd as _run

    a = {name: np.asarray(value) for name, value in inputs.items()}
    ins = {
        "x": np.ascontiguousarray(a["L0_attn_x"]),
        "attn": _pairs_of_heads(a["L0_attn_wq"], a["L0_attn_w_up"], a["L0_attn_wo"]),
        "ffn": _pairs_of_hidden(a["L0_ffn_w1"], a["L0_ffn_w3"], a["L0_ffn_w2"],
                                a["L0_ffn_sw1"], a["L0_ffn_sw3"], a["L0_ffn_sw2"]),
        "wdown": np.ascontiguousarray(a["L0_attn_w_down"]),
        "gate": np.ascontiguousarray(a["L0_ffn_gate_w"].T),
        **_constants(),
    }
    nc = _bacc.Bacc("TRN2", target_bir_lowering=False, num_devices=1)
    aps = {name: nc.dram_tensor(f"in_{name}", v.shape, mybir.dt.from_np(v.dtype), kind="ExternalInput").ap()
           for name, v in ins.items()}
    out = nc.dram_tensor("out", (B, T, D), F32, kind="ExternalOutput").ap()
    moe_attention_kernel(nc, aps["x"], aps["attn"], aps["ffn"], aps["wdown"], aps["gate"], aps["cos"],
                         aps["sin"], aps["mask"], aps["ident"], aps["iota"], aps["sel"], out)
    r = _run(nc, [{f"in_{name}": v for name, v in ins.items()}], core_ids=[0])
    return r.results[0]["out"]
```

```python
from contextlib import ExitStack

import concourse.bass as bass
import numpy as np
from concourse import mybir

B, T, D = 4, 512, 256
H, DH, DL = 16, 128, 128
E, HID, TOP_K = 8, 176, 2
ROUTED_SCALE = 2.5
ROPE_BASE = 10000.0
EPS = 1e-5
SCALE = DH ** -0.5
P = 128
KD = D // P
NT = T // P
TT = B * NT
PAIRS = H // 2
HIDDEN = (E + 1) * HID
HTILES = -(-HIDDEN // P)
FPAIRS = -(-HTILES // 2)
SLOTS = H * B
BODY = 16
LOOPS = 3
LEAD = 3
CPARTS = 3
BIG = 1e30

F32 = mybir.dt.float32
F32R = mybir.dt.float32r
BF16 = mybir.dt.bfloat16
U16 = mybir.dt.uint16
U32 = mybir.dt.uint32
ALU = mybir.AluOpType
ACT = mybir.ActivationFunctionType

WQ, WK, WUV, WO = 0, 512, 768, 1024
ATTN_COLS = 1536
W1, W3, W2 = 0, 512, 1024
FFN_COLS = 1536
PT_AT = [0, 512, 896, 1152]
PR_AT = [0, 128, 384, 768]
PROBS = 1280


def ffn_of(m):
    if m < 8 * (HTILES // 2):
        return m
    if m < 8 * FPAIRS and m % 2 == 0:
        return 8 * (HTILES // 2) + (m - 8 * (HTILES // 2)) // 2
    return None


def moe_attention_kernel(nc, x_d, attn_d, ffn_d, wdown_d, gate_d, cos_d, sin_d, mask_d, ident_d,
                         iota_d, sel_d, out_d):
    with ExitStack() as ctx:
        def sb(name, shape, dt=F32):
            return ctx.enter_context(nc.sbuf_tensor(name, shape, dt))

        def ps(name, shape):
            return ctx.enter_context(nc.psum_tensor(name, shape, F32))

        def sem(name):
            return ctx.enter_context(nc.semaphore(name))

        acc = sb("acc", [P, TT, D])
        xn_hi = sb("xn_hi", [P, KD, B * T], F32R)
        xn_lo = sb("xn_lo", [P, KD, B * T], F32R)
        ct_hi = sb("ct_hi", [P, B * T], F32R)
        ct_lo = sb("ct_lo", [P, B * T], F32R)
        c_hi = sb("c_hi", [P, TT, DL], F32R)
        c_lo = sb("c_lo", [P, TT, DL], F32R)
        combT = sb("combT", [CPARTS * (E + 1), B * T], BF16)
        cos_t = sb("cos_t", [P, T])
        sin_t = sb("sin_t", [P, T])
        mask = sb("mask", [P, T])
        ident = sb("ident", [P, P])
        raw_a = sb("raw_a", [P, ATTN_COLS])
        raw_f = sb("raw_f", [P, FFN_COLS])
        wa_hi = sb("wa_hi", [P, 2, WUV], F32R)
        wa_lo = sb("wa_lo", [P, 2, WUV], F32R)
        m_hi = sb("m_hi", [P, 2, 2 * D], F32R)
        m_lo = sb("m_lo", [P, 2, 2 * D], F32R)
        wf_hi = sb("wf_hi", [P, 2, FFN_COLS], F32R)
        wf_lo = sb("wf_lo", [P, 2, FFN_COLS], F32R)
        sel = sb("sel", [CPARTS * (E + 1), 2, 2 * P], U16)
        qk_hi = sb("qk_hi", [P, 2, 2, T], F32R)
        qk_lo = sb("qk_lo", [P, 2, 2, T], F32R)
        swapped = sb("swapped", [P, 2, T])
        rot = sb("rot", [P, 2, T])
        probs = sb("probs", [P, 2, PROBS])
        pt_hi = sb("pt_hi", [P, PROBS], F32R)
        pt_lo = sb("pt_lo", [P, PROBS], F32R)
        u_hi = sb("u_hi", [P, T], F32R)
        u_lo = sb("u_lo", [P, T], F32R)
        th = sb("th", [P, T])
        act = sb("act", [P, T])
        g_hi = sb("g_hi", [P, T], F32R)
        g_lo = sb("g_lo", [P, T], F32R)
        nbias = sb("nbias", [P, 2, NT])
        sums = sb("sums", [P, 2, NT])
        rsum = sb("rsum", [P, 2, NT])
        bn = sb("bn", [P, TT, 6])
        mv = sb("mv", [P, TT, 2])
        std = sb("std", [P, TT])
        rstd = sb("rstd", [P, 3, TT])
        gate_r = sb("gate_r", [P, KD, E])
        gate = sb("gate", [P, KD, 2 * E], F32R)
        iota = sb("iota", [P, E])
        top = sb("top", [P, TT, 8])
        topi = sb("topi", [P, TT, 8], U32)
        topf = sb("topf", [P, TT, 2])
        tsum = sb("tsum", [P, 2, TT])
        topw = sb("topw", [P, TT, 2])
        partb = sb("partb", [P, TT, CPARTS * (E + 1)], BF16)

        s_bank = [ps(f"scores{i}", [P, T]) for i in range(2)]
        pt_bank = ps("probs_t", [P, T])
        u_bank = ps("u_acc", [P, T])
        qk_bank = ps("qk_proj", [P, T])
        f_bank = ps("ffn", [P, T])
        out_bank = ps("out_acc", [P, NT, D])
        out_flat = out_bank[:, :, :].rearrange("p i d -> p (i d)")

        ld_x, ld_const = [sem(f"ld_x{b}") for b in range(B)], sem("ld_const")
        ld_table = sem("ld_table")
        ld_a, ld_f = sem("ld_a"), sem("ld_f")
        st_out = sem("st_out")
        stats, var_ok, std_ok = sem("stats"), sem("var_ok"), sem("std_ok")
        xn_ok, xt_ok, xhi_ok, xlo_ok = sem("xn_ok"), sem("xt_ok"), sem("xhi_ok"), sem("xlo_ok")
        wd_hi_ok, wd_lo_ok = sem("wd_hi_ok"), sem("wd_lo_ok")
        ct_ok, craw_ok, cthi_ok, ctlo_ok = sem("ct_ok"), sem("craw_ok"), sem("cthi_ok"), sem("ctlo_ok")
        c_ok, chi_ok, clo_ok = sem("c_ok"), sem("chi_ok"), sem("clo_ok")
        lt_ok, lrow_ok = sem("lt_ok"), sem("lrow_ok")
        logit_ok, lcopy_ok, sig_ok, tanh_ok = sem("logit_ok"), sem("lcopy_ok"), sem("sig_ok"), sem("tanh_ok")
        dve_step, part_ok, partT_ok, comb_ok = sem("dve_step"), sem("part_ok"), sem("partT_ok"), sem("comb_ok")
        wa_hi_ok, wa_lo_ok = sem("wa_hi_ok"), sem("wa_lo_ok")
        wf_hi_ok, wf_lo_ok = sem("wf_hi_ok"), sem("wf_lo_ok")
        m_ok, m_hi_ok, m_lo_ok = sem("m_ok"), sem("m_hi_ok"), sem("m_lo_ok")
        proj_ok, swap_ok, cosm_ok, sinm_ok = sem("proj_ok"), sem("swap_ok"), sem("cosm_ok"), sem("sinm_ok")
        rot_ok, rhi_ok, rlo_ok = sem("rot_ok"), sem("rhi_ok"), sem("rlo_ok")
        score_ok, max_ok, exp_ok, rsum_ok, prob_ok = (sem("score_ok"), sem("max_ok"), sem("exp_ok"),
                                                      sem("rsum_ok"), sem("prob_ok"))
        pt_ok, pthi_ok, ptlo_ok = sem("pt_ok"), sem("pthi_ok"), sem("ptlo_ok")
        u_ok, uhi_ok, ulo_ok = sem("u_ok"), sem("uhi_ok"), sem("ulo_ok")
        d_done, y_done, out_free = sem("d_done"), sem("y_done"), sem("out_free")
        h_ok, tanh_h_ok, gated_ok = sem("h_ok"), sem("tanh_h_ok"), sem("gated_ok")
        up_ok, upm_ok, cw_ok, g_ok = sem("up_ok"), sem("upm_ok"), sem("cw_ok"), sem("g_ok")
        ghi_ok, glo_ok = sem("ghi_ok"), sem("glo_ok")
        scores_seen = sem("scores_seen")
        N_CONST, N_TABLE = 4, 3

        wd_hi = pt_hi[:, 0:D].rearrange("p (k n) -> p k n", k=KD)
        wd_lo = pt_lo[:, 0:D].rearrange("p (k n) -> p k n", k=KD)
        wd_r = th[:, 0:D].rearrange("p (k n) -> p k n", k=KD)
        xn = probs[:, :, 0:4 * D].rearrange("p a (t d) -> p a t d", d=D)
        craw = swapped
        ct_banks = [u_bank[:, :], out_flat[:, T:2 * T]]
        comb = th[:, :].rearrange("p (k n) -> p k n", k=TOP_K)[:, :, 0:TT * (E + 1)].rearrange(
            "p k (t e) -> p k t e", t=TT)
        part = g_lo[:, 0:TT * CPARTS * (E + 1)].rearrange("p (t e) -> p t e", t=TT)
        logit_banks, logits_t = [f_bank, pt_bank], [act[:, :], probs[:, 1, 0:T]]
        score = th[:, D:].rearrange("p (t e) -> p t e", t=TT)

        def f32(ap):
            return ap.bitcast(F32)

        def need(eng, semaphore, value, fused=True):
            if isinstance(value, int):
                if value > 0:
                    eng.wait_ge(semaphore, value)
                return
            eng.wait_ge(semaphore, value)
            if not fused:
                eng.sem_inc(scores_seen)

        def run_slots(eng, slot):
            for s in range(-LEAD, 0):
                slot(0, s)
            with eng.Fori(0, LOOPS) as it:
                for s in range(BODY):
                    slot(it, s)
            for s in range(LOOPS * BODY, SLOTS):
                slot(0, s)

        def only(it, s, when, stage, *args):
            if isinstance(it, int) and s == when:
                stage(*args)

        def exists(it, m):
            return True if not isinstance(it, int) else 0 <= m < SLOTS

        def ffn(it, m):
            if not isinstance(it, int):
                return m
            return ffn_of(m) if exists(it, m) else None

        def at(it, per_slot, m):
            return it * (BODY * per_slot) + m * per_slot

        def pair_at(it, q):
            return it * 2 + q

        def prep(it, s):
            q, r = s // 8 + 1, s % 8
            if s < 0 or (isinstance(it, int) and q >= PAIRS):
                return None, None
            return q, r

        block = ctx.enter_context(nc.Block())

        @block.sync
        def _(sp):
            for b in range(B):
                sp.dma_start(acc[:, NT * b:NT * b + NT, :],
                             x_d[b].rearrange("(i p) d -> p i d", p=P)).then_inc(ld_x[b], 16)
                if b == 0:
                    sp.dma_start(ident[:, :], ident_d).then_inc(ld_const, 16)
                    sp.dma_start(wd_r, wdown_d.rearrange("(k p) n -> p k n", p=P)).then_inc(ld_const, 16)
                    sp.dma_start(gate_r[:, :, :], gate_d.rearrange("(k p) n -> p k n", p=P)).then_inc(ld_const, 16)
                    sp.dma_start(iota[:, :], iota_d).then_inc(ld_const, 16)
            sp.dma_start(raw_a[:, :], attn_d[0]).then_inc(ld_a, 16)
            sp.dma_start(cos_t[:, :], cos_d).then_inc(ld_table, 16)
            sp.dma_start(sin_t[:, :], sin_d).then_inc(ld_table, 16)
            sp.dma_start(mask[:, :], mask_d).then_inc(ld_table, 16)
            sp.dma_start(raw_f[:, :], ffn_d[0]).then_inc(ld_f, 16)
            sp.dma_start(sel[:, 0, :], sel_d[0]).then_inc(ld_f, 16)

            def attn_weights(p):
                sp.wait_ge(wa_hi_ok, p + 1)
                sp.wait_ge(wa_lo_ok, p + 1)
                sp.wait_ge(m_ok, p + 1)
                sp.dma_start(raw_a[:, :], attn_d[bass.ds(p + 1, 1)].rearrange("a p n -> p (a n)")).then_inc(ld_a, 16)

            def ffn_weights(p, parity):
                sp.wait_ge(wf_hi_ok, p + 1)
                sp.wait_ge(wf_lo_ok, p + 1)
                sp.dma_start(raw_f[:, :], ffn_d[bass.ds(p + 1, 1)].rearrange("a p n -> p (a n)")).then_inc(ld_f, 16)
                sp.wait_ge(cw_ok, 8 * p + 1)
                sp.dma_start(sel[:, parity, :], sel_d[bass.ds(p + 1, 1)].rearrange("a p n -> p (a n)")).then_inc(ld_f, 16)

            with sp.Fori(0, LOOPS) as it:
                for q in range(2):
                    attn_weights(it * 2 + q)
                    ffn_weights(it * 2 + q, (q + 1) % 2)
            attn_weights(2 * LOOPS)
            for b in range(B):
                sp.wait_ge(out_free, 1 + B * (PAIRS - 1) + b + 1)
                sp.dma_start(out_d[b].rearrange("(i p) d -> p i d", p=P),
                             acc[:, NT * b:NT * b + NT, :]).then_inc(st_out, 16)
            sp.wait_ge(st_out, 16 * B)

        @block.tensor
        def _(pe):
            def product(out, pairs, start, stop, **kw):
                n = 0
                for (a_hi, a_lo), (b_hi, b_lo) in pairs:
                    for a, b in ((a_hi, b_hi), (a_hi, b_lo), (a_lo, b_hi)):
                        last = pe.matmul(out, a, b, start=start and n == 0,
                                         stop=stop and n == 3 * len(pairs) - 1, **kw)
                        n += 1
                return last

            def value_output(parity):
                for hp in range(2):
                    last = pe.matmul(qk_bank[:, hp * D:hp * D + D], raw_a[:, WUV + hp * DL:WUV + hp * DL + DL],
                                     raw_a[:, WO + hp * D:WO + hp * D + D], start=True, stop=True)
                last.then_inc(m_ok, 1)

            def latent_rows(b):
                pe.wait_ge(craw_ok, b + 1)
                if b:
                    pe.wait_ge(clo_ok, b)
                for i in range(NT):
                    last = pe.transpose(out_flat[:, i * P:i * P + P], craw[:, b % 2, i * P:i * P + P], ident[:, :])
                last.then_inc(c_ok, 1)

            def logits(b):
                if b >= 2:
                    pe.wait_ge(lt_ok, b - 1)
                for n, (a, k) in enumerate((a, k) for a in (xn_hi, xn_lo) for k in range(KD)):
                    last = pe.matmul(logit_banks[b % 2][0:2 * E, :], gate[:, k, :], a[:, k, b * T:b * T + T],
                                     start=n == 0, stop=n == 3)
                last.then_inc(logit_ok, 1)

            def logit_rows(b):
                pe.wait_ge(lt_ok, b + 1)
                for i in range(NT):
                    t = NT * b + i
                    last = pe.transpose(u_bank[:, t * 2 * E:(t + 1) * 2 * E],
                                        logits_t[b % 2][0:2 * E, i * P:i * P + P], ident[0:2 * E, 0:2 * E])
                last.then_inc(lrow_ok, 1)

            pe.wait_ge(ld_const, 16 * N_CONST)
            banks = [s_bank, [pt_bank, qk_bank]]
            for b in range(B):
                for i in range(NT):
                    t = NT * b + i
                    pe.wait_ge(xn_ok, t + 1)
                    if b >= 2 and i == 0:
                        pe.wait_ge(xhi_ok, KD * (b - 1))
                        pe.wait_ge(xlo_ok, KD * (b - 1))
                    for k in range(KD):
                        last = pe.transpose(banks[b % 2][k][:, i * P:i * P + P],
                                            xn[:, t // 4 % 2, t % 4, k * P:k * P + P], ident[:, :])
                    last.then_inc(xt_ok, 1)
            pe.wait_ge(wd_hi_ok, 2)
            pe.wait_ge(wd_lo_ok, 2)
            for b in range(B):
                pe.wait_ge(xhi_ok, KD * (b + 1))
                pe.wait_ge(xlo_ok, KD * (b + 1))
                if b >= 2:
                    pe.wait_ge(ctlo_ok, b - 1)
                product(ct_banks[b % 2], [((wd_hi[:, k, :], wd_lo[:, k, :]),
                                                 (xn_hi[:, k, b * T:b * T + T], xn_lo[:, k, b * T:b * T + T]))
                                                for k in range(KD)], True, True).then_inc(ct_ok, 1)
                if b >= 1:
                    latent_rows(b - 1)
            pe.wait_ge(ld_a, 16)
            value_output(0)
            latent_rows(B - 1)
            pe.wait_ge(chi_ok, B)
            pe.wait_ge(clo_ok, B)
            pe.wait_ge(ctlo_ok, B)
            pe.wait_ge(m_hi_ok, 1)
            pe.wait_ge(m_lo_ok, 1)

            def combine_weights():
                pe.wait_ge(part_ok, 1)
                for b in range(B):
                    if b >= 2:
                        pe.wait_ge(comb_ok, b - 1)
                    c = (b + 1) % 2 * T
                    for i in range(NT):
                        last = pe.transpose(out_flat[0:CPARTS * (E + 1), c + i * P:c + i * P + P],
                                            f32(part[:, NT * b + i, :]), ident[:, :])
                    last.then_inc(partT_ok, 1)
                pe.wait_ge(comb_ok, B)

            def where(m):
                return (m // 8) % 2, (m % 8) // 2, m % 2

            def x_of(b):
                return [(xn_hi[:, k, b * T:b * T + T], xn_lo[:, k, b * T:b * T + T]) for k in range(KD)]

            def project(it, m, which):
                if not exists(it, m):
                    return
                par, b, hp = where(m)
                if m % 8 == 0 and which == 0:
                    need(pe, wa_hi_ok, pair_at(it, m // 8) + 1)
                    need(pe, wa_lo_ok, pair_at(it, m // 8) + 1)
                need(pe, swap_ok, at(it, 2, m) + which)
                need(pe, cosm_ok, at(it, 2, m) + which)
                if which == 0:
                    c = hp * DH
                    prods = [((wa_hi[:, par, WQ + 256 * k + c:WQ + 256 * k + c + DH],
                               wa_lo[:, par, WQ + 256 * k + c:WQ + 256 * k + c + DH]), x_of(b)[k])
                             for k in range(KD)]
                else:
                    c = WK + hp * DH
                    prods = [((wa_hi[:, par, c:c + DH], wa_lo[:, par, c:c + DH]),
                              (ct_hi[:, b * T:b * T + T], ct_lo[:, b * T:b * T + T]))]
                product(qk_bank[:, :], prods, True, True).then_inc(proj_ok, 1)

            def scores(it, m, i):
                if not exists(it, m):
                    return
                k = NT - 1 - i
                if k == 0:
                    need(pe, rhi_ok, at(it, 2, m + 1))
                    need(pe, rlo_ok, at(it, 2, m + 1))
                need(pe, exp_ok, at(it, 4, m) + k - 1)
                q, n = (m % 2, 0, slice(i * P, i * P + P)), (i + 1) * P
                product(s_bank[i % 2][:, 0:n],
                        [((qk_hi[:, q[0], 0, q[2]], qk_lo[:, q[0], 0, q[2]]),
                          (qk_hi[:, m % 2, 1, 0:n], qk_lo[:, m % 2, 1, 0:n]))], True, True).then_inc(score_ok, 1)

            def transposes(it, m, j):
                if not exists(it, m):
                    return
                if j == 0:
                    need(pe, prob_ok, at(it, 4, m + 1))
                need(pe, ptlo_ok, at(it, 4, m) + j)
                for i in range(j, NT):
                    a = PR_AT[i] + j * P
                    last = pe.transpose(pt_bank[:, (i - j) * P:(i - j + 1) * P], probs[:, m % 2, a:a + P],
                                        ident[:, :])
                last.then_inc(pt_ok, 1)

            def weighted(it, m, j):
                if not exists(it, m):
                    return
                if j == 0:
                    need(pe, uhi_ok, at(it, 1, m))
                    need(pe, ulo_ok, at(it, 1, m))
                need(pe, ptlo_ok, at(it, 4, m) + j + 1)
                _, b, _ = where(m)
                t, a, n = NT * b + j, PT_AT[j], T - j * P
                last = product(u_bank[:, j * P:T], [((c_hi[:, t, :], c_lo[:, t, :]),
                                                     (pt_hi[:, a:a + n], pt_lo[:, a:a + n]))], j == 0, j == NT - 1)
                if j == NT - 1:
                    last.then_inc(u_ok, 1)

            def out_products(parts, w_hi, w_lo, opens):
                a_hi, a_lo = parts
                for i in range(NT):
                    t = slice(i * P, i * P + P)
                    last = product(out_bank[:, i, :], [((a_hi[:, t], a_lo[:, t]), (w_hi, w_lo))],
                                   opens and i % 2 == 0, False, skip_group_check=True)
                return last

            def outputs(it, s):
                par, b, hp = where(s)
                even = s % 2 == 0
                f = ffn(it, s)

                def y():
                    if f is None:
                        return
                    need(pe, ghi_ok, at(it, 1, f + 1))
                    need(pe, glo_ok, at(it, 1, f + 1))
                    c = W2 + hp * D
                    out_products((g_hi, g_lo), wf_hi[:, par, c:c + D], wf_lo[:, par, c:c + D],
                                 False).then_inc(y_done, 1)

                def d():
                    if not exists(it, s):
                        return
                    if even:
                        need(pe, out_free, it * (BODY // 2) + s // 2 + 1)
                    if s % 8 == 0:
                        need(pe, m_hi_ok, pair_at(it, s // 8) + 1)
                        need(pe, m_lo_ok, pair_at(it, s // 8) + 1)
                    need(pe, uhi_ok, at(it, 1, s + 1))
                    need(pe, ulo_ok, at(it, 1, s + 1))
                    last = out_products((u_hi, u_lo), m_hi[:, par, hp * D:hp * D + D],
                                        m_lo[:, par, hp * D:hp * D + D], even)
                    last.then_inc(d_done, 1)
                return y, d

            def hidden(it, m, which):
                f = ffn(it, m)
                if f is None:
                    return
                par, b, hp = where(m)
                if m % 8 == 0 and which == 0:
                    need(pe, wf_hi_ok, pair_at(it, m // 8) + 1)
                    need(pe, wf_lo_ok, pair_at(it, m // 8) + 1)
                need(pe, g_ok, at(it, 1, f)) if which == 0 else need(pe, gated_ok, at(it, 1, f + 1))
                c = (W1, W3)[which] + hp * P
                product(f_bank[:, :], [((wf_hi[:, par, c + 256 * k:c + 256 * k + P],
                                         wf_lo[:, par, c + 256 * k:c + 256 * k + P]), x_of(b)[k])
                                       for k in range(KD)], True, True).then_inc((h_ok, up_ok)[which], 1)

            def combine(it, m):
                f = ffn(it, m)
                if f is None:
                    return
                par, b, hp = where(m)
                if m % 8 == 0:
                    need(pe, ld_f, pair_at(it, m // 8) * 32 + 32)
                need(pe, upm_ok, at(it, 1, f + 1))
                pe.matmul(f_bank[:, :], sel[:, par, hp * P:hp * P + P].bitcast(BF16),
                          combT[:, b * T:b * T + T], start=True, stop=True).then_inc(cw_ok, 1)

            def slot(it, s):
                y, d = outputs(it, s)
                q, r = prep(it, s)
                transposes(it, s + 1, 0)
                if r == 4:
                    need(pe, m_hi_ok, pair_at(it, q) + 1)
                    need(pe, m_lo_ok, pair_at(it, q) + 1)
                project(it, s + 3, 0)
                combine(it, s)
                only(it, s, -3, logits, 0)
                scores(it, s + 2, 3)
                transposes(it, s + 1, 1)
                only(it, s, -3, logits, 1)
                scores(it, s + 2, 2)
                weighted(it, s + 1, 0)
                d()
                transposes(it, s + 1, 2)
                scores(it, s + 2, 1)
                project(it, s + 3, 1)
                hidden(it, s + 1, 0)
                scores(it, s + 2, 0)
                only(it, s, -3, logit_rows, 0)
                only(it, s, -3, logits, 2)
                only(it, s, -3, logit_rows, 1)
                only(it, s, -3, logits, 3)
                only(it, s, -3, logit_rows, 2)
                only(it, s, -3, logit_rows, 3)
                transposes(it, s + 1, 3)
                weighted(it, s + 1, 1)
                y()
                weighted(it, s + 1, 2)
                if r == 3:
                    need(pe, cosm_ok, at(it, 2, s + 4))
                    need(pe, ld_a, (pair_at(it, q) + 1) * 16)
                    value_output(q % 2)
                only(it, s, -1, combine_weights)
                hidden(it, s + 1, 1)
                weighted(it, s + 1, 3)

            run_slots(pe, slot)

        @block.scalar
        def _(ac):
            def m_parts(p_count, parity):
                need(ac, m_ok, p_count)
                ac.activation(m_hi[:, parity, :], qk_bank[:, :], ACT.Copy).then_inc(m_hi_ok, 1)

            def std_of(g):
                ac.wait_ge(var_ok, g + 1)
                ac.activation(std[:, 8 * g:8 * g + 8], rstd[:, 0, 8 * g:8 * g + 8], ACT.Sqrt).then_inc(std_ok, 1)

            std_of(0)
            std_of(1)
            ac.wait_ge(ld_const, 16 * N_CONST)
            ac.activation(wd_hi, wd_r, ACT.Copy).then_inc(wd_hi_ok, 1)
            ac.activation(gate[:, :, 0:E], gate_r[:, :, :], ACT.Copy).then_inc(wd_hi_ok, 1)
            banks = [s_bank, [pt_bank, qk_bank]]
            for b in range(B):
                ac.wait_ge(xt_ok, NT * (b + 1))
                for k in range(KD):
                    ac.activation(xn_hi[:, k, b * T:b * T + T], banks[b % 2][k][:, :], ACT.Copy).then_inc(xhi_ok, 1)

            def latent_rows(b):
                ac.wait_ge(c_ok, b + 1)
                ac.activation(c_hi[:, NT * b:NT * b + NT, :].rearrange("p i d -> p (i d)"),
                              out_flat[:, 0:T], ACT.Copy).then_inc(chi_ok, 1)

            for b in range(B):
                ac.wait_ge(ct_ok, b + 1)
                if b >= 2:
                    ac.wait_ge(c_ok, b - 1)
                ac.activation(craw[:, b % 2, :], ct_banks[b % 2], ACT.Copy).then_inc(craw_ok, 1)
                ac.activation(ct_hi[:, b * T:b * T + T], ct_banks[b % 2], ACT.Copy).then_inc(cthi_ok, 1)
                if b >= 1:
                    latent_rows(b - 1)
            ac.wait_ge(ld_a, 16)
            ac.activation(wa_hi[:, 0, :], raw_a[:, 0:WUV], ACT.Copy).then_inc(wa_hi_ok, 1)
            m_parts(1, 0)
            latent_rows(B - 1)
            ac.wait_ge(ld_f, 32)
            ac.activation(wf_hi[:, 0, :], raw_f[:, :], ACT.Copy).then_inc(wf_hi_ok, 1)

            def copy_logits(b):
                ac.wait_ge(logit_ok, b + 1)
                if b >= 2:
                    ac.wait_ge(lrow_ok, b - 1)
                ac.activation(logits_t[b % 2][0:2 * E, :], logit_banks[b % 2][0:2 * E, :], ACT.Copy).then_inc(lt_ok, 1)

            def gate_scores():
                ac.wait_ge(lrow_ok, B)
                ac.activation(score[:, :, :].rearrange("p t e -> p (t e)"), u_bank[:, 0:TT * 2 * E],
                              ACT.Copy).then_inc(lcopy_ok, 1)
                ac.wait_ge(sig_ok, 1)
                ac.activation(score[:, :, E:2 * E], score[:, :, 0:E], ACT.Tanh, scale=0.5).then_inc(tanh_ok, 1)

            def combine_weights():
                for b in range(B):
                    ac.wait_ge(partT_ok, b + 1)
                    c = (b + 1) % 2 * T
                    ac.activation(combT[:, b * T:b * T + T], out_flat[0:CPARTS * (E + 1), c:c + T],
                                  ACT.Copy).then_inc(comb_ok, 1)

            def swap(it, m, which):
                if not exists(it, m):
                    return
                need(ac, proj_ok, at(it, 2, m) + which + 1)
                need(ac, rot_ok, at(it, 2, m - 1) + which + 1)
                for half in range(2):
                    last = ac.activation(swapped[64 * half:64 * half + 64, which, :],
                                         qk_bank[64 - 64 * half:128 - 64 * half, :], ACT.Copy)
                last.then_inc(swap_ok, 1)

            def rot_parts(it, m, which):
                if not exists(it, m):
                    return
                need(ac, rot_ok, at(it, 2, m) + which + 1)
                need(ac, score_ok, at(it, 4, m - 1))
                ac.activation(qk_hi[:, m % 2, which, :], rot[:, which, :], ACT.Copy).then_inc(rhi_ok, 1)

            def exps(it, m, i):
                if not exists(it, m):
                    return
                k = NT - 1 - i
                need(ac, max_ok, at(it, 4, m) + k + 1)
                if k == 0:
                    need(ac, pt_ok, at(it, 4, m - 1))
                n = (i + 1) * P
                ac.activation(probs[:, m % 2, PR_AT[i]:PR_AT[i] + n], s_bank[i % 2][:, 0:n], ACT.Exp,
                              bias=nbias[:, m % 2, i:i + 1], scale=-1.0,
                              accum_out=sums[:, m % 2, i:i + 1]).then_inc(exp_ok, 1)

            def pt_parts(it, m, j):
                if not exists(it, m):
                    return
                if j == 0:
                    need(ac, u_ok, at(it, 1, m))
                need(ac, pt_ok, at(it, 4, m) + j + 1)
                n = T - j * P
                ac.activation(pt_hi[:, PT_AT[j]:PT_AT[j] + n], pt_bank[:, 0:n], ACT.Copy).then_inc(pthi_ok, 1)

            def u_parts(it, m):
                if not exists(it, m):
                    return
                need(ac, d_done, at(it, 1, m))
                need(ac, u_ok, at(it, 1, m + 1))
                ac.activation(u_hi[:, :], u_bank[:, :], ACT.Copy).then_inc(uhi_ok, 1)

            def tanh(it, m):
                f = ffn(it, m)
                if f is None:
                    return
                need(ac, gated_ok, at(it, 1, f))
                need(ac, h_ok, at(it, 1, f + 1))
                ac.activation(th[:, :], f_bank[:, :], ACT.Tanh, scale=0.5).then_inc(tanh_h_ok, 1)

            def g_parts(it, m):
                f = ffn(it, m)
                if f is None:
                    return
                need(ac, y_done, at(it, 1, f))
                need(ac, g_ok, at(it, 1, f + 1))
                ac.activation(g_hi[:, :], act[:, :], ACT.Copy).then_inc(ghi_ok, 1)

            def weights(it, s):
                q, r = prep(it, s)
                if r not in (2, 3, 4):
                    return
                if r == 2:
                    need(ac, d_done, at(it, 1, 8 * (q - 1) + 2))
                    need(ac, ld_a, (pair_at(it, q) + 1) * 16)
                    ac.activation(wa_hi[:, q % 2, :], raw_a[:, 0:WUV], ACT.Copy).then_inc(wa_hi_ok, 1)
                if r == 3:
                    m_parts(pair_at(it, q) + 1, q % 2)
                if r == 4 and (not isinstance(it, int) or q < FPAIRS):
                    need(ac, ld_f, (pair_at(it, q) + 1) * 32)
                    ac.activation(wf_hi[:, q % 2, :], raw_f[:, :], ACT.Copy).then_inc(wf_hi_ok, 1)

            def slot(it, s):
                u_parts(it, s)
                pt_parts(it, s + 1, 0)
                swap(it, s + 3, 0)
                pt_parts(it, s + 1, 1)
                exps(it, s + 2, 3)
                g_parts(it, s)
                only(it, s, -3, copy_logits, 0)
                only(it, s, -3, copy_logits, 1)
                rot_parts(it, s + 3, 0)
                pt_parts(it, s + 1, 2)
                exps(it, s + 2, 2)
                swap(it, s + 3, 1)
                only(it, s, -3, copy_logits, 2)
                exps(it, s + 2, 1)
                tanh(it, s + 1)
                only(it, s, -1, combine_weights)
                pt_parts(it, s + 1, 3)
                exps(it, s + 2, 0)
                weights(it, s)
                only(it, s, -3, copy_logits, 3)
                only(it, s, -3, gate_scores)
                rot_parts(it, s + 3, 1)

            run_slots(ac, slot)

        @block.gpsimd
        def _(pool):
            def parts_of(p_count_a, parity):
                need(pool, wa_hi_ok, p_count_a)
                pool.tensor_tensor(wa_lo[:, parity, :], raw_a[:, 0:WUV], f32(wa_hi[:, parity, :]),
                                   ALU.subtract).then_inc(wa_lo_ok, 1)

            def ffn_parts(part_no, parity, p_count):
                need(pool, wf_hi_ok, p_count)
                c = slice(512 * part_no, 512 * part_no + 512)
                ins = pool.tensor_tensor(wf_lo[:, parity, c], raw_f[:, c], f32(wf_hi[:, parity, c]), ALU.subtract)
                if part_no == 2:
                    ins.then_inc(wf_lo_ok, 1)

            pool.wait_ge(ld_table, 16 * N_TABLE)
            parts_of(1, 0)

            def first_ffn_parts():
                for n in range(3):
                    ffn_parts(n, 0, 1)

            def sin_product(it, m, which):
                if not exists(it, m):
                    return
                need(pool, swap_ok, at(it, 2, m) + which + 1)
                pool.tensor_tensor(swapped[:, which, :], swapped[:, which, :], sin_t[:, :],
                                   ALU.mult).then_inc(sinm_ok, 1)

            def rot_parts(it, m, which):
                if not exists(it, m):
                    return
                need(pool, rhi_ok, at(it, 2, m) + which + 1)
                pool.tensor_tensor(qk_lo[:, m % 2, which, :], rot[:, which, :], f32(qk_hi[:, m % 2, which, :]),
                                   ALU.subtract).then_inc(rlo_ok, 1)

            def g_parts(it, m):
                f = ffn(it, m)
                if f is None:
                    return
                need(pool, ghi_ok, at(it, 1, f + 1))
                pool.tensor_tensor(g_lo[:, :], act[:, :], f32(g_hi[:, :]), ALU.subtract).then_inc(glo_ok, 1)

            def weights(it, s):
                q, r = prep(it, s)
                if r == 2:
                    parts_of(pair_at(it, q) + 1, q % 2)
                if r in (4, 5, 6) and (not isinstance(it, int) or q < FPAIRS):
                    ffn_parts(r - 4, q % 2, pair_at(it, q) + 1)

            def slot(it, s):
                sin_product(it, s + 3, 0)
                g_parts(it, s)
                sin_product(it, s + 3, 1)
                rot_parts(it, s + 3, 0)
                rot_parts(it, s + 3, 1)
                only(it, s, -2, first_ffn_parts)
                weights(it, s)

            run_slots(pool, slot)

        @block.vector
        def _(ve):
            steps = [0]

            def step(ins):
                steps[0] += 1
                ins.then_inc(dve_step, 1)
                ve.wait_ge(dve_step, steps[0])

            def flat(ap):
                return ap.rearrange("p t e -> p (t e)")

            def variance(g):
                for b in (2 * g, 2 * g + 1):
                    ve.wait_ge(ld_x[b], 16)
                    for t in range(NT * b, NT * b + NT):
                        last = ve.bn_stats(bn[:, t, :], acc[:, t, :])
                    last.then_inc(stats, 1)
                    ve.wait_ge(stats, b + 1)
                    for t in range(NT * b, NT * b + NT):
                        last = ve.bn_aggr(mv[:, t, :], bn[:, t, :])
                step(last)
                ve.tensor_scalar(rstd[:, 0, 8 * g:8 * g + 8], mv[:, 8 * g:8 * g + 8, 1], EPS, None,
                                 ALU.add).then_inc(var_ok, 1)

            def inverse_std(g):
                v, r, n = (rstd[:, k, 8 * g:8 * g + 8] for k in range(3))
                ve.wait_ge(std_ok, g + 1)
                step(ve.reciprocal(r, std[:, 8 * g:8 * g + 8]))
                step(ve.tensor_tensor(n, v, r, ALU.mult))
                step(ve.tensor_tensor(n, n, r, ALU.mult))
                step(ve.tensor_scalar(n, n, -0.5, 1.5, ALU.mult, ALU.add))
                step(ve.tensor_tensor(v, n, r, ALU.mult))

            def normalised(b):
                for t in range(NT * b, NT * b + NT):
                    if t >= 8:
                        ve.wait_ge(xt_ok, t - 7)
                    ve.tensor_scalar(xn[:, t // 4 % 2, t % 4, :], acc[:, t, :], mv[:, t, 0:1],
                                     rstd[:, 0, t:t + 1], ALU.subtract, ALU.mult).then_inc(xn_ok, 1)

            variance(0)
            inverse_std(0)
            normalised(0)
            normalised(1)
            variance(1)
            inverse_std(1)
            banks = [s_bank, [pt_bank, qk_bank]]

            def x_low(b):
                for k in range(KD):
                    ve.wait_ge(xhi_ok, KD * b + k + 1)
                    ve.tensor_tensor(xn_lo[:, k, b * T:b * T + T], banks[b % 2][k][:, :],
                                     f32(xn_hi[:, k, b * T:b * T + T]), ALU.subtract).then_inc(xlo_ok, 1)

            x_low(0)
            normalised(2)
            x_low(1)
            normalised(3)
            ve.wait_ge(wd_hi_ok, 2)
            ve.tensor_tensor(wd_lo, wd_r, f32(wd_hi), ALU.subtract).then_inc(wd_lo_ok, 1)
            ve.tensor_tensor(gate[:, :, E:2 * E], gate_r[:, :, :], f32(gate[:, :, 0:E]),
                             ALU.subtract).then_inc(wd_lo_ok, 1)
            ve.wait_ge(wd_lo_ok, 2)
            ve.memset(comb[:, 0, :, :], 0.5).then_inc(out_free, 1)
            x_low(2)
            x_low(3)

            def latent_rows(b):
                ve.wait_ge(chi_ok, b + 1)
                ve.tensor_tensor(flat(c_lo[:, NT * b:NT * b + NT, :]), out_flat[:, 0:T],
                                 f32(flat(c_hi[:, NT * b:NT * b + NT, :])), ALU.subtract).then_inc(clo_ok, 1)

            for b in range(B):
                ve.wait_ge(cthi_ok, b + 1)
                ve.tensor_tensor(ct_lo[:, b * T:b * T + T], ct_banks[b % 2],
                                 f32(ct_hi[:, b * T:b * T + T]), ALU.subtract).then_inc(ctlo_ok, 1)
                if b >= 1:
                    latent_rows(b - 1)

            def m_parts(p_count, parity):
                need(ve, m_hi_ok, p_count)
                ve.tensor_tensor(m_lo[:, parity, :], qk_bank[:, :], f32(m_hi[:, parity, :]),
                                 ALU.subtract).then_inc(m_lo_ok, 1)

            m_parts(1, 0)
            latent_rows(B - 1)
            ve.wait_ge(ld_table, 16 * N_TABLE)

            def logit_sums():
                ve.wait_ge(lcopy_ok, 1)
                ve.tensor_tensor(score[:, :, 0:E], score[:, :, 0:E], score[:, :, E:2 * E],
                                 ALU.add).then_inc(sig_ok, 1)

            def best_experts():
                ve.wait_ge(tanh_ok, 1)
                step(ve.tensor_scalar(score[:, :, 0:E], score[:, :, E:2 * E], 0.5, 0.5, ALU.mult, ALU.add))
                for t in range(TT):
                    last = ve.max(top[:, t, :], score[:, t, 0:E])
                step(last)
                for t in range(TT):
                    last = ve.max_index(topi[:, t, :], top[:, t, :], score[:, t, 0:E])
                step(last)

            def best_weights():
                ve.tensor_copy(topf[:, :, :], topi[:, :, 0:TOP_K])
                step(ve.tensor_tensor(tsum[:, 0, :], top[:, :, 0], top[:, :, 1], ALU.add))
                step(ve.tensor_scalar(tsum[:, 0, :], tsum[:, 0, :], 1e-20, None, ALU.add))
                step(ve.reciprocal(tsum[:, 1, :], tsum[:, 0, :]))
                for k in range(TOP_K):
                    last = ve.scalar_tensor_tensor(out=topw[:, :, k], in0=top[:, :, k], scalar=0.5 * ROUTED_SCALE,
                                                   in1=tsum[:, 1, :], op0=ALU.mult, op1=ALU.mult)
                step(last)

            def combine_weights():
                all_t = [P, TT, E]
                for k in range(TOP_K):
                    last = ve.tensor_tensor(comb[:, k, :, 0:E], iota[:, :].unsqueeze(1).to_broadcast(all_t),
                                            topf[:, :, k:k + 1].to_broadcast(all_t), ALU.is_equal)
                step(last)
                for k in range(TOP_K):
                    last = ve.tensor_tensor(comb[:, k, :, 0:E], comb[:, k, :, 0:E],
                                            topw[:, :, k:k + 1].to_broadcast(all_t), ALU.mult)
                step(last)
                step(ve.tensor_tensor(comb[:, 0, :, 0:E], comb[:, 0, :, 0:E], comb[:, 1, :, 0:E], ALU.add))
                for n in range(CPARTS):
                    c = slice(n * (E + 1), (n + 1) * (E + 1))
                    step(ve.tensor_copy(partb[:, :, c], comb[:, 0, :, :]))
                    last = ve.tensor_copy(part[:, :, c], partb[:, :, c])
                    if n < CPARTS - 1:
                        step(last)
                        step(ve.tensor_tensor(comb[:, 0, :, :], comb[:, 0, :, :], f32(part[:, :, c]), ALU.subtract))
                last.then_inc(part_ok, 1)

            def cos_product(it, m, which):
                if not exists(it, m):
                    return
                need(ve, swap_ok, at(it, 2, m) + which + 1)
                need(ve, rlo_ok, at(it, 2, m - 1) + which + 1)
                ve.tensor_tensor(rot[:, which, :], qk_bank[:, :], cos_t[:, :], ALU.mult).then_inc(cosm_ok, 1)

            def rotate(it, m, which):
                if not exists(it, m):
                    return
                need(ve, cosm_ok, at(it, 2, m) + which + 1)
                need(ve, sinm_ok, at(it, 2, m) + which + 1)
                ve.tensor_tensor(rot[:, which, :], rot[:, which, :], swapped[:, which, :],
                                 ALU.add).then_inc(rot_ok, 1)

            def row_max(it, m, i):
                if not exists(it, m):
                    return
                need(ve, score_ok, at(it, 4, m) + NT - i, fused=False)
                n = (i + 1) * P
                s = s_bank[i % 2][:, 0:n]
                ve.tensor_tensor_reduce(s, s, mask[:, T - n:T], -SCALE, 3e38, ALU.add, ALU.min,
                                        nbias[:, m % 2, i:i + 1]).then_inc(max_ok, 1)

            def invert_sum(it, m, i):
                if not exists(it, m):
                    return
                need(ve, exp_ok, at(it, 4, m) + NT - i)
                ve.reciprocal(rsum[:, m % 2, i:i + 1], sums[:, m % 2, i:i + 1]).then_inc(rsum_ok, 1)

            def normalise(it, m, i):
                if not exists(it, m):
                    return
                need(ve, rsum_ok, at(it, 4, m) + NT - i)
                a = probs[:, m % 2, PR_AT[i]:PR_AT[i] + (i + 1) * P]
                ve.tensor_scalar(a, a, rsum[:, m % 2, i:i + 1], None, ALU.mult).then_inc(prob_ok, 1)

            def pt_parts(it, m, j):
                if not exists(it, m):
                    return
                need(ve, pthi_ok, at(it, 4, m) + j + 1)
                n = T - j * P
                c = slice(PT_AT[j], PT_AT[j] + n)
                ve.tensor_tensor(pt_lo[:, c], pt_bank[:, 0:n], f32(pt_hi[:, c]), ALU.subtract).then_inc(ptlo_ok, 1)

            def u_parts(it, m):
                if not exists(it, m):
                    return
                need(ve, uhi_ok, at(it, 1, m + 1))
                ve.tensor_tensor(u_lo[:, :], u_bank[:, :], f32(u_hi[:, :]), ALU.subtract).then_inc(ulo_ok, 1)

            def gate_h(it, m):
                f = ffn(it, m)
                if f is None:
                    return
                need(ve, tanh_h_ok, at(it, 1, f + 1))
                need(ve, glo_ok, at(it, 1, f))
                ve.scalar_tensor_tensor(out=act[:, :], in0=th[:, :], scalar=1.0, in1=f_bank[:, :],
                                        op0=ALU.add, op1=ALU.mult).then_inc(gated_ok, 1)

            def times_bank(it, m, filled, before, after):
                f = ffn(it, m)
                if f is None:
                    return
                need(ve, before, at(it, 1, f + 1))
                need(ve, filled, at(it, 1, f + 1))
                ve.tensor_tensor(act[:, :], act[:, :], f_bank[:, :], ALU.mult).then_inc(after, 1)

            def add_out(it, s):
                if not exists(it, s) or s % 2 == 0:
                    return
                b = (s % 8) // 2
                need(ve, d_done, at(it, 1, s + 1))
                if ffn(it, s) is not None:
                    need(ve, y_done, at(it, 1, s + 1))
                elif ffn(it, s - 1) is not None:
                    need(ve, y_done, ffn(it, s - 1) + 1)
                need(ve, out_free, it * (BODY // 2) + s // 2 + 1)
                a = flat(acc[:, NT * b:NT * b + NT, :])
                ve.tensor_tensor(a, a, out_flat, ALU.add).then_inc(out_free, 1)

            def slot(it, s):
                q, r = prep(it, s)
                times_bank(it, s, up_ok, gated_ok, upm_ok)
                pt_parts(it, s + 1, 0)
                only(it, s, -1, combine_weights)
                u_parts(it, s)
                times_bank(it, s, cw_ok, upm_ok, g_ok)
                only(it, s, -2, logit_sums)
                cos_product(it, s + 3, 0)
                only(it, s, -2, best_experts)
                row_max(it, s + 2, 3)
                pt_parts(it, s + 1, 1)
                rotate(it, s + 3, 0)
                row_max(it, s + 2, 2)
                invert_sum(it, s + 2, 3)
                normalise(it, s + 2, 3)
                pt_parts(it, s + 1, 2)
                only(it, s, -2, best_weights)
                invert_sum(it, s + 2, 2)
                row_max(it, s + 2, 1)
                normalise(it, s + 2, 2)
                row_max(it, s + 2, 0)
                cos_product(it, s + 3, 1)
                invert_sum(it, s + 2, 1)
                gate_h(it, s + 1)
                pt_parts(it, s + 1, 3)
                normalise(it, s + 2, 1)
                invert_sum(it, s + 2, 0)
                normalise(it, s + 2, 0)
                rotate(it, s + 3, 1)
                if r == 3:
                    m_parts(pair_at(it, q) + 1, q % 2)
                add_out(it, s)

            run_slots(ve, slot)

def _pairs_of_heads(wq, w_up, wo):
    halves = np.concatenate([np.arange(0, DH, 2), np.arange(1, DH, 2)])
    blob = np.zeros((PAIRS, P, ATTN_COLS), wq.dtype)
    q = wq.reshape(KD, P, PAIRS, 2, DH)[..., halves]
    blob[:, :, WQ:WK] = q.transpose(2, 1, 0, 3, 4).reshape(PAIRS, P, -1)
    kv = w_up.reshape(DL, PAIRS, 2, 2, DH)
    blob[:, :, WK:WUV] = kv[:, :, :, 0, :][..., halves].transpose(1, 0, 2, 3).reshape(PAIRS, P, -1)
    blob[:, :, WUV:WO] = kv[:, :, :, 1, :].transpose(1, 3, 2, 0).reshape(PAIRS, P, -1)
    blob[:, :, WO:] = wo.reshape(PAIRS, 2, DH, D).transpose(0, 2, 1, 3).reshape(PAIRS, P, -1)
    return blob


def _pairs_of_hidden(w1, w3, w2, sw1, sw3, sw2):
    n = FPAIRS * 2 * P
    up = np.zeros((2, D, n), w1.dtype)
    down = np.zeros((n, D), w1.dtype)
    for e in range(E + 1):
        at = slice(e * HID, (e + 1) * HID)
        up[0, :, at], up[1, :, at], down[at] = (w1[e], w3[e], w2[e]) if e < E else (sw1, sw3, sw2)
    blob = np.zeros((FPAIRS, P, FFN_COLS), w1.dtype)
    u = up.reshape(2, KD, P, FPAIRS, 2 * P).transpose(3, 2, 0, 1, 4)
    blob[:, :, W1:W2] = u.reshape(FPAIRS, P, -1)
    blob[:, :, W2:] = down.reshape(FPAIRS, 2, P, D).transpose(0, 2, 1, 3).reshape(FPAIRS, P, -1)
    return blob


def _constants():
    freq = (1.0 / ROPE_BASE ** (np.arange(0, DH, 2, dtype=np.float32) / DH)).astype(np.float32)
    ang = (np.arange(T, dtype=np.float32)[None, :] * freq[:, None]).astype(np.float32)
    cos = np.concatenate([np.cos(ang), np.cos(ang)]).astype(np.float32)
    sin = np.concatenate([-np.sin(ang), np.sin(ang)]).astype(np.float32)
    mask = np.zeros((P, T), np.float32)
    mask[:, T - P:] = np.where(np.arange(P)[:, None] >= np.arange(P)[None, :], 0.0, -BIG)
    iota = np.tile(np.arange(E, dtype=np.float32), (P, 1))
    owner = np.arange(FPAIRS * 2 * P) // HID
    chosen = (owner[None, :] == np.arange(E + 1)[:, None])
    bf16_one = np.uint16(0x3F80)
    sel = np.where(np.tile(chosen, (CPARTS, 1)), bf16_one, np.uint16(0))
    sel = sel.reshape(CPARTS * (E + 1), FPAIRS, 2 * P).transpose(1, 0, 2)
    return {"cos": cos, "sin": sin, "mask": mask, "ident": np.eye(P, dtype=np.float32),
            "iota": iota, "sel": np.ascontiguousarray(sel)}


def kernel(**inputs):
    import concourse.bacc as _bacc
    from concourse.bass_utils import run_bass_kernel_spmd as _run

    a = {name: np.asarray(value) for name, value in inputs.items()}
    ins = {
        "x": np.ascontiguousarray(a["L0_attn_x"]),
        "attn": _pairs_of_heads(a["L0_attn_wq"], a["L0_attn_w_up"], a["L0_attn_wo"]),
        "ffn": _pairs_of_hidden(a["L0_ffn_w1"], a["L0_ffn_w3"], a["L0_ffn_w2"],
                                a["L0_ffn_sw1"], a["L0_ffn_sw3"], a["L0_ffn_sw2"]),
        "wdown": np.ascontiguousarray(a["L0_attn_w_down"]),
        "gate": np.ascontiguousarray(a["L0_ffn_gate_w"].T),
        **_constants(),
    }
    nc = _bacc.Bacc("TRN2", target_bir_lowering=False, num_devices=1)
    aps = {name: nc.dram_tensor(f"in_{name}", v.shape, mybir.dt.from_np(v.dtype), kind="ExternalInput").ap()
           for name, v in ins.items()}
    out = nc.dram_tensor("out", (B, T, D), F32, kind="ExternalOutput").ap()
    moe_attention_kernel(nc, aps["x"], aps["attn"], aps["ffn"], aps["wdown"], aps["gate"], aps["cos"],
                         aps["sin"], aps["mask"], aps["ident"], aps["iota"], aps["sel"], out)
    r = _run(nc, [{f"in_{name}": v for name, v in ins.items()}], core_ids=[0])
    return r.results[0]["out"]
```
